# Optimizing a Trainium2 kernel written in Bass

```python
import numpy as np
import jax
import jax.numpy as jnp

def _softmax(x, axis=-1):
    return jax.nn.softmax(x, axis=axis)

def _gelu(x):
    return jax.nn.gelu(x, approximate=True)

def _silu(x):
    return jax.nn.silu(x)

def _sigmoid(x):
    return jax.nn.sigmoid(x)

def _layernorm(x, axis=-1, eps=1e-05):
    m = jnp.mean(x, axis=axis, keepdims=True)
    v = jnp.var(x, axis=axis, keepdims=True)
    return (x - m) / jnp.sqrt(v + eps)

def _scatter_add(tgt, idx, src, axis=0):
    return tgt.at[idx].add(src)

def _segment_sum(src, seg, n):
    return jax.ops.segment_sum(src, seg, n)
kernel_name = 'mk_seq_preln_d1_jaxref_r4_5f5f25'

def setup_inputs(seed: int=0):
    np.random.seed(seed)
    _w = jnp.asarray

    def _L0_attn_setup():
        import jax, jax.numpy as jnp
        import numpy as np
        from jax import lax
        D_MODEL = 512
        D_INNER = 1024
        D_CONV = 4
        B, T = (4, 512)

        def _rmsnorm(h):
            n = jnp.sqrt(jnp.sum(h * h, axis=-1, keepdims=True))
            return h / jnp.maximum(n, 1e-12) * h.shape[-1] ** 0.5

        def _mamba_fallback(h, W_in, conv_w, conv_b, W_out):
            xz = jnp.einsum('btd,ed->bte', h, W_in)
            xp, z = jnp.split(xz, 2, axis=-1)
            xc = lax.conv_general_dilated(xp.transpose(0, 2, 1), conv_w, window_strides=(1,), padding=[(D_CONV - 1, 0)], dimension_numbers=('NCH', 'OIH', 'NCH'), feature_group_count=D_INNER) + conv_b[None, :, None]
            xc = xc.transpose(0, 2, 1)
            y = jax.nn.silu(xc) * jax.nn.silu(z)
            return jnp.einsum('bte,de->btd', y, W_out)
        key = jax.random.key(seed)
        ks = jax.random.split(key, 7)
        std = 0.02
        return {'x': jax.random.normal(ks[0], (B, T, D_MODEL), jnp.float32), 'W_in': jax.random.normal(ks[1], (2 * D_INNER, D_MODEL), jnp.float32) * std, 'conv_w': jax.random.normal(ks[2], (D_INNER, 1, D_CONV), jnp.float32) * std, 'conv_b': jnp.zeros((D_INNER,), jnp.float32), 'W_out': jax.random.normal(ks[3], (D_MODEL, D_INNER), jnp.float32) * std, 'W_mlp1': jax.random.normal(ks[4], (4 * D_MODEL, D_MODEL), jnp.float32) * std, 'W_mlp2': jax.random.normal(ks[5], (D_MODEL, 4 * D_MODEL), jnp.float32) * std}
    _L0_attn_in = _L0_attn_setup()

    def _L0_ffn_setup():
        import jax, jax.numpy as jnp
        import numpy as np
        E = 16
        D = 512
        H = 352
        HS = 2 * 352
        TOP_K = 6
        ROUTE_SCALE = 1.0
        key = jax.random.key(seed)
        ks = jax.random.split(key, 16)
        s = 0.02
        return {'x': jax.random.normal(ks[0], (4, 256, D), dtype=jnp.float32), 'gate_w': jax.random.normal(ks[1], (E, D), dtype=jnp.float32) * s, 'gate_b': jax.random.normal(ks[2], (E,), dtype=jnp.float32) * s, 'w1': jax.random.normal(ks[3], (E, H, D), dtype=jnp.float32) * s, 'b1': jax.random.normal(ks[4], (E, H), dtype=jnp.float32) * s, 'w2': jax.random.normal(ks[5], (E, D, H), dtype=jnp.float32) * s, 'b2': jax.random.normal(ks[6], (E, D), dtype=jnp.float32) * s, 'w3': jax.random.normal(ks[7], (E, H, D), dtype=jnp.float32) * s, 'b3': jax.random.normal(ks[8], (E, H), dtype=jnp.float32) * s, 'ws1': jax.random.normal(ks[9], (HS, D), dtype=jnp.float32) * s, 'bs1': jax.random.normal(ks[10], (HS,), dtype=jnp.float32) * s, 'ws2': jax.random.normal(ks[11], (D, HS), dtype=jnp.float32) * s, 'bs2': jax.random.normal(ks[12], (D,), dtype=jnp.float32) * s, 'ws3': jax.random.normal(ks[13], (HS, D), dtype=jnp.float32) * s, 'bs3': jax.random.normal(ks[14], (HS,), dtype=jnp.float32) * s}
    _L0_ffn_in = _L0_ffn_setup()
    _d = {'L0_attn_x': _L0_attn_in['x'], 'L0_attn_W_in': _L0_attn_in['W_in'], 'L0_attn_conv_w': _L0_attn_in['conv_w'], 'L0_attn_conv_b': _L0_attn_in['conv_b'], 'L0_attn_W_out': _L0_attn_in['W_out'], 'L0_attn_W_mlp1': _L0_attn_in['W_mlp1'], 'L0_attn_W_mlp2': _L0_attn_in['W_mlp2'], 'L0_ffn_gate_w': _L0_ffn_in['gate_w'], 'L0_ffn_gate_b': _L0_ffn_in['gate_b'], 'L0_ffn_w1': _L0_ffn_in['w1'], 'L0_ffn_b1': _L0_ffn_in['b1'], 'L0_ffn_w2': _L0_ffn_in['w2'], 'L0_ffn_b2': _L0_ffn_in['b2'], 'L0_ffn_w3': _L0_ffn_in['w3'], 'L0_ffn_b3': _L0_ffn_in['b3'], 'L0_ffn_ws1': _L0_ffn_in['ws1'], 'L0_ffn_bs1': _L0_ffn_in['bs1'], 'L0_ffn_ws2': _L0_ffn_in['ws2'], 'L0_ffn_bs2': _L0_ffn_in['bs2'], 'L0_ffn_ws3': _L0_ffn_in['ws3'], 'L0_ffn_bs3': _L0_ffn_in['bs3']}
    _x0 = _d['L0_attn_x']
    _d['L0_attn_x'] = jax.random.normal(jax.random.fold_in(jax.random.key(seed), 1), (4, 512, 512), dtype=_x0.dtype)
    del _x0
    return _d

def reference(L0_attn_x, L0_attn_W_in, L0_attn_conv_w, L0_attn_conv_b, L0_attn_W_out, L0_attn_W_mlp1, L0_attn_W_mlp2, L0_ffn_gate_w, L0_ffn_gate_b, L0_ffn_w1, L0_ffn_b1, L0_ffn_w2, L0_ffn_b2, L0_ffn_w3, L0_ffn_b3, L0_ffn_ws1, L0_ffn_bs1, L0_ffn_ws2, L0_ffn_bs2, L0_ffn_ws3, L0_ffn_bs3):

    def _L0_attn_ref(x, W_in, conv_w, conv_b, W_out, W_mlp1, W_mlp2):
        import jax, jax.numpy as jnp
        import numpy as np
        from jax import lax
        D_MODEL = 512
        D_INNER = 1024
        D_CONV = 4
        B, T = (4, 512)

        def _rmsnorm(h):
            n = jnp.sqrt(jnp.sum(h * h, axis=-1, keepdims=True))
            return h / jnp.maximum(n, 1e-12) * h.shape[-1] ** 0.5

        def _mamba_fallback(h, W_in, conv_w, conv_b, W_out):
            xz = jnp.einsum('btd,ed->bte', h, W_in)
            xp, z = jnp.split(xz, 2, axis=-1)
            xc = lax.conv_general_dilated(xp.transpose(0, 2, 1), conv_w, window_strides=(1,), padding=[(D_CONV - 1, 0)], dimension_numbers=('NCH', 'OIH', 'NCH'), feature_group_count=D_INNER) + conv_b[None, :, None]
            xc = xc.transpose(0, 2, 1)
            y = jax.nn.silu(xc) * jax.nn.silu(z)
            return jnp.einsum('bte,de->btd', y, W_out)
        h = _rmsnorm(x)
        x = x + _mamba_fallback(h, W_in, conv_w, conv_b, W_out)
        h = _rmsnorm(x)
        m = jnp.einsum('bte,de->btd', jax.nn.relu(jnp.einsum('btd,ed->bte', h, W_mlp1)), W_mlp2)
        return x + m

    def _L0_ffn_ref(x, gate_w, gate_b, w1, b1, w2, b2, w3, b3, ws1, bs1, ws2, bs2, ws3, bs3):
        import jax, jax.numpy as jnp
        import numpy as np
        E = 16
        D = 512
        H = 352
        HS = 2 * 352
        TOP_K = 6
        ROUTE_SCALE = 1.0
        shape = x.shape
        xf = x.reshape(-1, shape[-1])
        scores = xf @ gate_w.T
        probs = jax.nn.softmax(scores.astype(jnp.float32), axis=-1)
        biased = probs + gate_b
        _, idx = jax.lax.top_k(biased, TOP_K)
        weights = jnp.take_along_axis(probs, idx, axis=1) * ROUTE_SCALE
        weights = weights.astype(x.dtype)
        onehot = jax.nn.one_hot(idx, E, dtype=weights.dtype)
        cw = jnp.einsum('tk,tke->te', weights, onehot)

        def expert_step(y, params):
            W1, B1, W2, B2, W3, B3, c = params
            h = jax.nn.silu(xf @ W1.T + B1) * (xf @ W3.T + B3)
            out = h @ W2.T + B2
            return (y + c[:, None] * out, None)
        y0 = jnp.zeros_like(xf)
        y, _ = jax.lax.scan(expert_step, y0, (w1, b1, w2, b2, w3, b3, cw.T))
        z = jax.nn.silu(xf @ ws1.T + bs1) * (xf @ ws3.T + bs3) @ ws2.T + bs2
        return (y + z).reshape(shape)
    x = L0_attn_x
    x = x + _L0_attn_ref(_layernorm(x, axis=-1), L0_attn_W_in, L0_attn_conv_w, L0_attn_conv_b, L0_attn_W_out, L0_attn_W_mlp1, L0_attn_W_mlp2)
    x = x + _L0_ffn_ref(_layernorm(x, axis=-1), L0_ffn_gate_w, L0_ffn_gate_b, L0_ffn_w1, L0_ffn_b1, L0_ffn_w2, L0_ffn_b2, L0_ffn_w3, L0_ffn_b3, L0_ffn_ws1, L0_ffn_bs1, L0_ffn_ws2, L0_ffn_bs2, L0_ffn_ws3, L0_ffn_bs3)
    return x

_drawn_inputs = setup_inputs


def setup_inputs(seed=0):
    import zlib

    import numpy as np

    out = dict(_drawn_inputs(seed))
    spreads = {'L0_attn_conv_b': (0.0, 0.8)}
    factors = {'L0_attn_W_in': 8.0,
     'L0_attn_conv_w': 8.0,
     'L0_attn_W_out': 8.0,
     'L0_ffn_gate_w': 8.0,
     'L0_ffn_gate_b': 8.0,
     'L0_ffn_w1': 8.0,
     'L0_ffn_b1': 25.444,
     'L0_ffn_w2': 8.0,
     'L0_ffn_b2': 196.486,
     'L0_ffn_w3': 8.0,
     'L0_ffn_b3': 26.255,
     'L0_ffn_bs1': 64.0,
     'L0_ffn_bs2': 146.506,
     'L0_ffn_bs3': 64.0,
     'L0_ffn_ws1': 8.0,
     'L0_ffn_ws2': 8.0,
     'L0_ffn_ws3': 8.0}
    for name, (base, spread) in spreads.items():
        noise = np.random.default_rng([zlib.crc32(name.encode()), seed]).standard_normal(out[name].shape)
        drawn = base * np.exp(spread * noise) if base else spread * noise
        out[name] = jnp.asarray(drawn.astype(out[name].dtype))
    for name, factor in factors.items():
        out[name] = (out[name] * factor).astype(out[name].dtype)
    return out
```

```python
from contextlib import ExitStack

import concourse.bass as bass
from concourse import mybir

F32 = mybir.dt.float32
F16 = mybir.dt.float16
ALU = mybir.AluOpType
ACT = mybir.ActivationFunctionType
AX = mybir.AxisListType

P = 128
D = 512
KD = D // P
T = 2048
NB = 4
TB = T // NB
NT = TB // P
TAPS = 4
E = 16
TOP = 6
HE = 352
SHARED = 2
SUB = 32
HROWS = -(-(E + SHARED) * HE // (5 * P)) * 5 * P
WS = 64.0
EPS = 1e-5
FLOOR = -3.0e38
TAKEN = -3.3e38
MIX, MLP, MOE = range(3)

UP = 2 * KD * P
COLS = {MIX: UP + D, MLP: UP + 2 * D, MOE: UP + D}
UNITS = {MIX: 4, MLP: 4, MOE: 5}
GROUPS = {MIX: 2, MLP: 2, MOE: HROWS // (5 * P)}
WCOLS = max(UNITS[p] * COLS[p] for p in COLS)
PASSES = ((0, 0), (0, 1), (1, 0))
HSLOTS = 4
CSLOTS = UNITS[MOE]

N_MOE = NB * UNITS[MOE]
PAIR = 2 * N_MOE
PAIRS = GROUPS[MOE] // 2


def plan():
    units = [(ph, g, b, c) for ph in (MIX, MLP) for g in range(2) for b in range(NB) for c in range(4)]
    at = {u: n for n, u in enumerate(units)}
    steps = [("prep", 0)] + [("split", w) for w in range(4)] + [("T", 0, 0, 0), ("T", 0, 0, 1)]
    after = {n: [] for n in range(len(units))}
    for b in range(NB - 1):
        after[at[MIX, 0, b, 0]].append(("prep", b + 1))
        after[at[MIX, 0, b, 2]] += [("T", 0, b + 1, h) for h in range(2)]
    for b in range(NB):
        nxt = (MIX, 1, b + 1, 2) if b + 1 < NB else (MLP, 0, 0, 2)
        after[at[nxt]] += [("T", 1, b, h) for h in range(2)]
    late = []
    for b in range(NB):
        todo = [[("T", 2, b, h) for h in range(2)], [("G", b)], [("W", b)], [("B", b, h) for h in range(2)]]
        for j, steps_j in enumerate(todo):
            n = at[MLP, 1, b, 2] + 4 + j
            if n in after:
                after[n] += steps_j
            else:
                late += steps_j
    for group in range(4):
        first = 4 * (group + 1)
        count = UNITS[MOE] if group == 3 else 4
        for w, slot in zip(range(first, first + count), (3, 6, 9, 12, 14)):
            after[16 * group + slot].append(("split", w))

    def down(n):
        out = [("D", n)]
        if units[n][3] == 3:
            out.append(("evac", n))
        return out

    for n in range(len(units)):
        if n >= 2:
            steps += down(n - 2)
        steps += [("U", n)] + after[n]
    steps += down(len(units) - 2) + down(len(units) - 1) + late
    return units, steps


def layer(nc, x, w_mix, w_mlp, w_moe, conv, gate_w, gate_b, out_bias, out):
    units, steps = plan()
    items = [s for s in steps if s[0] in "TUGWB"]
    item_of = {s: n for n, s in enumerate(items)}
    N_ITEMS = len(items)
    N_UNITS = len(units)
    N_SPLITS = 16
    N_RUNS = N_UNITS // 4
    assert N_ITEMS % 2 == 0 and N_UNITS % HSLOTS == 0 and PAIR % HSLOTS == 0

    crep = nc.dram_tensor("combine_rows", [HROWS // SUB, T], F32, kind="Internal").ap()

    with ExitStack() as ctx:
        def sb(name, shape, dt=F32):
            return ctx.enter_context(nc.sbuf_tensor(name, shape, dt))

        def sem(name):
            return ctx.enter_context(nc.semaphore(name))

        weights = sb("weights", [P, 2, 2, WCOLS], F16)
        xt = sb("xt", [P, NB, 2, KD, TB], F16)
        acc = sb("acc", [P, NB, NT, D])
        staged = sb("staged", [P, 2, COLS[MLP]])
        hidden = sb("hidden", [P, HSLOTS, 2, 2, TB], F16)
        shared_mem = sb("shared_mem", [P, 2 * NT * D])
        xin = shared_mem[:, 0:NT * D].rearrange("p (t d) -> p t d", t=NT)
        nat = shared_mem[:, NT * D:2 * NT * D].rearrange("p (t d) -> p t d", t=NT)
        cw_rows = shared_mem[:, 0:CSLOTS * TB].rearrange("p (s t) -> p s t", s=CSLOTS)
        tmp = sb("tmp", [P, 2, TB])
        sil = sb("sil", [P, 2, TB])
        h32 = sb("h32", [P, TB])
        xpad = sb("xpad", [P, 2, TAPS - 1 + TB + 1])
        ident = sb("ident", [P, P])
        convp = sb("convp", [P, 8, TAPS + 1])
        stats = sb("stats", [P, NT, 6])
        mv = sb("mv", [P, NT, 2])
        small = sb("small", [P, 4, NT])
        gate32 = sb("gate32", [P, KD, E])
        gate16 = sb("gate16", [P, 2, KD, E], F16)
        gbias = sb("gbias", [P, E])
        score = sb("score", [P, NT, E])
        prob = sb("prob", [P, NT, E])
        biased = sb("biased", [P, NT, E + 2])
        marked = sb("marked", [P, NT, E + 2])
        best = sb("best", [P, NT, 8])
        cw = sb("cw", [P, NT, E])
        cwt = sb("cwt", [E + 1, TB])
        cws = sb("cws", [E, TB])
        ob = sb("ob", [E + 1, D])
        inv = sb("inv", [SHARED * HE // SUB, T // 4])
        ebias = sb("ebias", [P, 2, UNITS[MOE], 2])

        ring = ctx.enter_context(nc.psum_tensor("ring", [P, 4, TB], F32))
        downs = ctx.enter_context(nc.psum_tensor("downs", [P, NT, D], F32))

        w_loaded = [sem(f"w_loaded{i}") for i in range(2)]
        cw_loaded = [sem(f"cw_loaded{i}") for i in range(CSLOTS)]
        x_loaded = sem("x_loaded")
        const_loaded = sem("const_loaded")
        cw_stored = sem("cw_stored")
        out_stored = sem("out_stored")
        ident_ready = sem("ident_ready")
        pool_step = sem("pool_step")
        filled = sem("filled")
        tile_done = sem("tile_done")
        w_high = sem("w_high")
        sqrt_done = sem("sqrt_done")
        exp_done = sem("exp_done")
        gate_high = sem("gate_high")
        t_high = sem("t_high")
        xp_ready = sem("xp_ready")
        silu_ready = sem("silu_ready")
        conv_silu = sem("conv_silu")
        h_high = sem("h_high")
        w_ready = sem("w_ready")
        freed = sem("freed")
        sqrt_in = sem("sqrt_in")
        exp_in = sem("exp_in")
        x_used = sem("x_used")
        nat_ready = sem("nat_ready")
        gate_ready = sem("gate_ready")
        cw_ready = sem("cw_ready")
        conv_ready = sem("conv_ready")
        h32_ready = sem("h32_ready")
        h_ready = sem("h_ready")
        acc_added = sem("acc_added")
        dve_step = sem("dve_step")

        def split_place(w):
            return ((MIX, MLP)[w // 8], w // 4 % 2, w % 4) if w < 16 else (MOE, 0, w - 16)

        def split_after(w):
            return NT * 16 * max(0, w // 4 - 1) if w < 16 else NT * 16 * 3

        def t_item(n, b, h):
            return item_of[("T", n, b, h)]

        split_slots = {g * N_MOE + 3 * j + 3: g * 5 + j for g in range(2) for j in range(5)}

        block = ctx.enter_context(nc.Block())

        @block.sync
        def _(sp):
            def load_x(b):
                sp.dma_start(xin, x[b * TB:(b + 1) * TB, :].rearrange("(t p) d -> p t d", p=P)).then_inc(x_loaded, 16)

            def load_w(w, source):
                if w >= 2:
                    sp.wait_ge(w_ready, w - 1)
                sp.dma_start(staged[:, w % 2, 0:source.shape[-1]], source).then_inc(w_loaded[w % 2], 16)

            load_x(0)
            for dst, src in ((convp[:], conv), (gate32[:], gate_w), (gbias[:], gate_b.partition_broadcast(P)),
                             (ob[:], out_bias)):
                sp.dma_start(dst, src).then_inc(const_loaded, 16)
            x_after = {3: 1, 4: 2, 5: 3, 10: 4, 17: 5, 18: 6, 19: 7}
            for w in range(21):
                load_w(w, w_mix[w] if w < 8 else w_mlp[w - 8] if w < 16 else w_moe[w - 16])
                if w in x_after:
                    n = x_after[w]
                    sp.wait_ge(x_used, n)
                    load_x(n % NB)
            n_rest = GROUPS[MOE] * UNITS[MOE] - 5
            with sp.Fori(0, n_rest - 1, 2) as j:
                for s in range(2):
                    sp.wait_ge(w_ready, j + (20 + s))
                    sp.dma_start(staged[:, (21 + s) % 2, 0:COLS[MOE] + 2],
                                 w_moe[bass.ds(j + (5 + s), 1), :, :].rearrange("a p n -> (a p) n")
                                 ).then_inc(w_loaded[(21 + s) % 2], 16)
            load_w(16 + GROUPS[MOE] * UNITS[MOE] - 1, w_moe[GROUPS[MOE] * UNITS[MOE] - 1])
            for b in range(NB):
                for t in range(NT):
                    sp.wait_ge(acc_added, NT * (N_RUNS + (GROUPS[MOE] - 1) * NB + b) + t + 1)
                    r = b * TB + t * P
                    sp.dma_start(out[r:r + P, :], acc[:, b, t, :]).then_inc(out_stored, 16)
            sp.wait_ge(out_stored, 16 * NB * NT)

        @block.gpsimd
        def _(pool):
            pool.memset(ident[:], 0.0).then_inc(pool_step, 1)
            pool.wait_ge(pool_step, 1)
            pool.affine_select(out=ident[:], in_=ident[:], compare_op=ALU.not_equal, fill=1.0, base=0,
                               pattern=[[-1, P]], channel_multiplier=1).then_inc(ident_ready, 1)
            pool.memset(inv[:], 1.0 / WS).then_inc(pool_step, 1)
            pool.wait_ge(pool_step, 2)
            n_shared, n_routed = SHARED * HE // SUB, E * HE // SUB
            n_zero = HROWS // SUB - n_shared - n_routed
            for q in range(4):
                cols = slice(q * (T // 4), (q + 1) * (T // 4))
                pool.dma_start(crep[0:n_shared, cols], inv[:]).then_inc(cw_stored, 16)
                pool.dma_start(crep[n_shared + n_routed:, cols], inv[0:n_zero, :]).then_inc(cw_stored, 16)
            for b in range(NB):
                pool.wait_ge(freed, item_of[("W", b)] + 1)
                rows = crep[n_shared:n_shared + n_routed, b * TB:(b + 1) * TB]
                pool.dma_start(rows.rearrange("(e r) t -> e r t", r=HE // SUB),
                               cws[:].unsqueeze(1).to_broadcast([E, HE // SUB, TB])).then_inc(cw_stored, 16)
                pool.wait_ge(cw_stored, 16 * (9 + b))
            pool.wait_ge(freed, N_ITEMS)
            table = crep.rearrange("(j q) t -> j q t", q=P // SUB)
            with pool.Fori(0, GROUPS[MOE]) as g:
                for b in range(NB):
                    for c in range(CSLOTS):
                        pool.wait_ge(h_ready, g * N_MOE + (32 + b * CSLOTS + c - CSLOTS + 1))
                        src = table[bass.ds(g * UNITS[MOE] + c, 1), :, b * TB:(b + 1) * TB]
                        src = src.rearrange("a q t -> (a q) t").unsqueeze(1).to_broadcast([P // SUB, SUB, TB])
                        pool.dma_start(cw_rows[:, c, :], src).then_inc(cw_loaded[c], 16)

        @block.tensor
        def _(pe):
            def up(slot, buf, base, b):
                for m in range(2):
                    for k in range(KD):
                        w0 = base + (m * KD + k) * P
                        for n, (pw, px) in enumerate(PASSES):
                            mm = pe.matmul(ring[:, 2 * slot + m, :], weights[:, buf, pw, w0:w0 + P],
                                           xt[:, b, px, k, :], start=(k == 0 and n == 0),
                                           stop=(k == KD - 1 and n == 2))
                    mm.then_inc(filled, 1)

            def down(hslot, chunks, buf, base, first, last, run):
                for t in range(NT):
                    if first and not (isinstance(run, int) and run == 0):
                        pe.wait_ge(acc_added, run * NT + (t + 1 - NT))
                    for c in range(chunks):
                        w0 = base + UP + c * D
                        for n, (ph, pw) in enumerate(PASSES):
                            mm = pe.matmul(downs[:, t, :], hidden[:, hslot, ph, c, t * P:(t + 1) * P],
                                           weights[:, buf, pw, w0:w0 + D], start=(first and c == 0 and n == 0),
                                           stop=(last and c == chunks - 1 and n == 2))
                    mm.then_inc(tile_done, 1)

            def slot_for(item):
                if item >= 2:
                    pe.wait_ge(freed, item - 1)
                return item % 2

            pe.wait_ge(ident_ready, 1)
            for step in steps:
                kind = step[0]
                if kind == "T":
                    _, n, b, h = step
                    s = slot_for(item_of[step])
                    pe.wait_ge(nat_ready, NB * n + b + 1)
                    for k in range(2):
                        for t in range(NT):
                            d0 = (2 * h + k) * P
                            tr = pe.transpose(ring[:, 2 * s + k, t * P:(t + 1) * P], nat[:, t, d0:d0 + P], ident[:])
                        tr.then_inc(filled, 1)
                elif kind == "U":
                    ph, g, b, c = units[step[1]]
                    s = slot_for(item_of[step])
                    if g == 0 and c == 0:
                        pe.wait_ge(freed, t_item(ph, b, 1) + 1)
                    if b == 0:
                        pe.wait_ge(w_ready, 8 * ph + 4 * g + c + 1)
                    up(s, g % 2, c * COLS[ph], b)
                elif kind == "D":
                    u = step[1]
                    ph, g, b, c = units[u]
                    if ph == MIX:
                        pe.wait_ge(h_ready, u + 1)
                    else:
                        pe.wait_ge(freed, item_of[("U", u)] + 1)
                    down(u % HSLOTS, 1 + (ph == MLP), g % 2, c * COLS[ph], c == 0, c == 3, u // 4)
                elif kind == "G":
                    b = step[1]
                    s = slot_for(item_of[step])
                    pe.wait_ge(freed, t_item(2, b, 1) + 1)
                    pe.wait_ge(gate_ready, 1)
                    for t in range(NT):
                        for k in range(KD):
                            for n, (px, pw) in enumerate(PASSES):
                                mm = pe.matmul(ring[:, 2 * s + t // 2, t % 2 * E:(t % 2 + 1) * E],
                                               xt[:, b, px, k, t * P:(t + 1) * P], gate16[:, pw, k, :],
                                               start=(k == 0 and n == 0), stop=(k == KD - 1 and n == 2))
                        if t % 2:
                            mm.then_inc(filled, 1)
                elif kind == "W":
                    b = step[1]
                    s = slot_for(item_of[step])
                    pe.wait_ge(cw_ready, b + 1)
                    for t in range(NT):
                        tr = pe.transpose(ring[0:E, 2 * s + t // 2, t % 2 * P:(t % 2 + 1) * P], cw[:, t, :], ident[:])
                        if t % 2:
                            tr.then_inc(filled, 1)
                elif kind == "B":
                    _, b, h = step
                    s = slot_for(item_of[step])
                    pe.wait_ge(freed, item_of[("W", b)] + 1)
                    pe.wait_ge(const_loaded, 64)
                    for t in range(2):
                        t0 = (2 * h + t) * P
                        pe.matmul(ring[:, 2 * s + t, :], cwt[:, t0:t0 + P], ob[:],
                                  start=True, stop=True).then_inc(filled, 1)

            def up_moe(m0, w0, k):
                pe.wait_ge(freed, m0 + (N_ITEMS + k - 1))
                if k % N_MOE < UNITS[MOE]:
                    pe.wait_ge(w_ready, w0 + (16 + k // N_MOE * UNITS[MOE] + k % N_MOE + 1))
                up(k % 2, k // N_MOE % 2, k % UNITS[MOE] * COLS[MOE], k % N_MOE // UNITS[MOE])

            def down_moe(m0, r0, k):
                pe.wait_ge(h_ready, m0 + (32 + k + 1))
                c = k % UNITS[MOE]
                down(k % HSLOTS, 1, k // N_MOE % 2, c * COLS[MOE], c == 0, c == UNITS[MOE] - 1,
                     r0 + (N_RUNS + k // UNITS[MOE]))

            up_moe(0, 0, 0)
            up_moe(0, 0, 1)
            with pe.Fori(0, PAIRS - 1) as i:
                for k in range(PAIR):
                    down_moe(i * PAIR, i * (PAIR // UNITS[MOE]), k)
                    up_moe(i * PAIR, i * (2 * UNITS[MOE]), k + 2)
            last = PAIRS - 1
            for k in range(PAIR):
                down_moe(last * PAIR, last * PAIR // UNITS[MOE], k)
                if k + 2 < PAIR:
                    up_moe(last * PAIR, last * 2 * UNITS[MOE], k + 2)

        @block.scalar
        def _(act):
            def split_high(w_slot, loads, free_at, buf, base, cols):
                act.wait_ge(w_loaded[w_slot], 16 * loads)
                if free_at is not None:
                    act.wait_ge(tile_done, free_at)
                act.activation(weights[:, buf, 0, base:base + cols], staged[:, w_slot, 0:cols], ACT.Copy,
                               scale=WS).then_inc(w_high, 1)

            roots = 0
            exps = 0
            halves = 0
            act.wait_ge(const_loaded, 64)
            act.activation(gate16[:, 0], gate32[:], ACT.Copy, scale=WS).then_inc(gate_high, 1)
            for step in steps:
                kind = step[0]
                if kind == "split":
                    w = step[1]
                    ph, buf, j = split_place(w)
                    split_high(w % 2, w // 2 + 1, split_after(w) or None, buf, j * COLS[ph], COLS[ph])
                elif kind == "prep":
                    for _ in range(2):
                        roots += 1
                        act.wait_ge(sqrt_in, roots)
                        act.activation(small[:, 1, :], small[:, 0, :], ACT.Sqrt).then_inc(sqrt_done, 1)
                elif kind == "T":
                    _, n, b, h = step
                    s = item_of[step] % 2
                    act.wait_ge(filled, 2 * item_of[step] + 2)
                    act.activation(xt[:, b, 0, 2 * h:2 * h + 2, :], ring[:, 2 * s:2 * s + 2, :],
                                   ACT.Copy).then_inc(t_high, 1)
                elif kind == "U":
                    u = step[1]
                    ph, g, b, c = units[u]
                    item = item_of[step]
                    s = item % 2
                    if ph == MIX:
                        act.wait_ge(filled, 2 * item + 1)
                        if u >= 2:
                            act.wait_ge(conv_ready, u - 1)
                        act.activation(xpad[:, u % 2, TAPS - 1:TAPS - 1 + TB], ring[:, 2 * s, :], ACT.Copy,
                                       scale=1 / WS).then_inc(xp_ready, 1)
                        act.wait_ge(filled, 2 * item + 2)
                        if u >= 2:
                            act.wait_ge(h32_ready, u - 1)
                        act.activation(sil[:, u % 2, :], ring[:, 2 * s + 1, :], ACT.Silu,
                                       scale=1 / WS).then_inc(silu_ready, 1)
                        act.wait_ge(conv_ready, u + 1)
                        act.activation(tmp[:, u % 2, :], tmp[:, u % 2, :], ACT.Silu).then_inc(conv_silu, 1)
                        act.wait_ge(h32_ready, u + 1)
                        if u >= HSLOTS:
                            act.wait_ge(tile_done, NT * (u - HSLOTS + 1))
                        act.activation(hidden[:, u % HSLOTS, 0, 0, :], h32[:], ACT.Copy).then_inc(h_high, 1)
                    else:
                        act.wait_ge(filled, 2 * item + 2)
                        act.wait_ge(tile_done, NT * (u - HSLOTS + 1))
                        act.activation(hidden[:, u % HSLOTS, 0, :, :], ring[:, 2 * s:2 * s + 2, :],
                                       ACT.Relu).then_inc(h_high, 1)
                elif kind == "evac":
                    ph, g, b, c = units[step[1]]
                    for _ in range(0 if g == 0 else 1):
                        roots += 1
                        act.wait_ge(sqrt_in, roots)
                        act.activation(small[:, 1, :], small[:, 0, :], ACT.Sqrt).then_inc(sqrt_done, 1)
                elif kind == "G":
                    exps += 1
                    act.wait_ge(exp_in, exps)
                    act.activation(prob[:], score[:], ACT.Exp).then_inc(exp_done, 1)

            def unit_moe(m0, k):
                s = k % 2
                act.wait_ge(filled, m0 * 2 + (2 * (N_ITEMS + k) + 1))
                act.activation(sil[:, s, :], ring[:, 2 * s, :], ACT.Silu, scale=1 / WS,
                               bias=ebias[:, k // N_MOE % 2, k % UNITS[MOE], 0:1]).then_inc(silu_ready, 1)
                act.wait_ge(h32_ready, m0 + (32 + k + 1))
                act.wait_ge(tile_done, m0 * NT + NT * (N_UNITS + k - HSLOTS + 1))
                act.activation(hidden[:, k % HSLOTS, 0, 0, :], h32[:], ACT.Copy).then_inc(h_high, 1)

            def split_moe(m0, l0, j):
                w = 21 + j
                split_high(w % 2, l0 + (w // 2 + 1), m0 * NT + NT * (N_UNITS + (j // 5) * N_MOE),
                           (1 + j // 5) % 2, j % 5 * COLS[MOE], COLS[MOE])

            def turn(i, n_splits):
                for k in range(PAIR):
                    unit_moe(i * PAIR, k)
                    j = split_slots.get(k)
                    if j is not None and j < n_splits:
                        split_moe(i * PAIR, i * UNITS[MOE], j)

            with act.Fori(0, PAIRS - 1) as i:
                turn(i, 10)
            turn(PAIRS - 1, 5)

        @block.vector
        def _(dve):
            steps_done = [0]

            def link(ins):
                steps_done[0] += 1
                ins.then_inc(dve_step, 1)
                dve.wait_ge(dve_step, steps_done[0])

            roots = 0

            def root():
                dve.wait_ge(sqrt_done, roots)

            def low_part(w_slot, buf, base, cols, high):
                dve.wait_ge(w_high, high)
                dve.scalar_tensor_tensor(out=weights[:, buf, 1, base:base + cols], in0=staged[:, w_slot, 0:cols],
                                         scalar=WS, in1=weights[:, buf, 0, base:base + cols], op0=ALU.mult,
                                         op1=ALU.subtract).then_inc(w_ready, 1)

            def up_bias(w_slot, buf, j):
                dve.tensor_copy(ebias[:, buf, j, 0:1], staged[:, w_slot, COLS[MOE]:COLS[MOE] + 1])
                dve.tensor_scalar(ebias[:, buf, j, 1:2], staged[:, w_slot, COLS[MOE] + 1:COLS[MOE] + 2], WS, None,
                                  ALU.mult)

            def nat_free(n, b):
                if n or b:
                    before = (n, b - 1) if b else (n - 1, NB - 1)
                    dve.wait_ge(filled, 2 * t_item(*before, 1) + 2)

            def layer_norm(src, dst, ends):
                nonlocal roots
                for t in range(NT):
                    ins = dve.bn_stats(stats[:, t, :], src[:, t, :])
                link(ins)
                for t in range(NT):
                    ins = dve.bn_aggr(mv[:, t, :], stats[:, t, :])
                link(ins)
                dve.tensor_scalar(small[:, 0, :], mv[:, :, 1], EPS, None, ALU.add).then_inc(sqrt_in, 1)
                roots += 1
                root()
                link(dve.reciprocal(small[:, 2, :], small[:, 1, :]))
                for t in range(NT):
                    ins = dve.tensor_scalar(dst[:, t, :], src[:, t, :], mv[:, t, 0:1], small[:, 2, t:t + 1],
                                            ALU.subtract, ALU.mult)
                ins.then_inc(ends, 1)

            def rms_norm(src):
                nonlocal roots
                for t in range(NT):
                    ins = dve.tensor_tensor_reduce(nat[:, t, :], src[:, t, :], src[:, t, :], 1.0, 0.0, ALU.mult, ALU.add,
                                                   small[:, 0, t:t + 1])
                ins.then_inc(sqrt_in, 1)
                roots += 1
                root()
                link(dve.tensor_scalar(small[:, 2, :], small[:, 1, :], 1e-12, None, ALU.max))
                link(dve.reciprocal(small[:, 3, :], small[:, 2, :]))
                for t in range(NT):
                    ins = dve.tensor_scalar(nat[:, t, :], src[:, t, :], small[:, 3, t:t + 1], float(D) ** 0.5,
                                            ALU.mult, ALU.mult)
                ins.then_inc(nat_ready, 1)

            dve.memset(xpad[:], 0.0)
            dve.memset(biased[:], FLOOR)
            link(dve.memset(cwt[:], 1.0))
            dve.wait_ge(gate_high, 1)
            dve.scalar_tensor_tensor(out=gate16[:, 1], in0=gate32[:], scalar=WS, in1=gate16[:, 0], op0=ALU.mult,
                                     op1=ALU.subtract).then_inc(gate_ready, 1)
            for step in steps:
                kind = step[0]
                if kind == "split":
                    w = step[1]
                    ph, buf, j = split_place(w)
                    if ph == MOE:
                        dve.wait_ge(w_high, w + 1)
                        up_bias(w % 2, buf, j)
                    low_part(w % 2, buf, j * COLS[ph], COLS[ph], w + 1)
                elif kind == "prep":
                    b = step[1]
                    dve.wait_ge(x_loaded, 16 * (b + 1))
                    layer_norm(xin, acc[:, b], x_used)
                    dve.wait_ge(x_used, b + 1)
                    nat_free(0, b)
                    rms_norm(acc[:, b])
                elif kind == "T":
                    _, n, b, h = step
                    s = item_of[step] % 2
                    dve.wait_ge(t_high, 2 * (NB * n + b) + h + 1)
                    dve.tensor_tensor(xt[:, b, 1, 2 * h:2 * h + 2, :], ring[:, 2 * s:2 * s + 2, :],
                                      xt[:, b, 0, 2 * h:2 * h + 2, :], ALU.subtract).then_inc(freed, 1)
                elif kind == "U":
                    u = step[1]
                    ph, g, b, c = units[u]
                    item = item_of[step]
                    s = item % 2
                    if ph == MIX:
                        cc = 4 * g + c
                        dve.wait_ge(xp_ready, u + 1)
                        dve.wait_ge(silu_ready, u + 1)
                        dve.tensor_scalar(tmp[:, u % 2, :], xpad[:, u % 2, TAPS - 1:TAPS - 1 + TB],
                                          convp[:, cc, TAPS - 1:TAPS], convp[:, cc, TAPS:TAPS + 1], ALU.mult,
                                          ALU.add).then_inc(freed, 1)
                        dve.wait_ge(freed, item + 1)
                        for tap in range(TAPS - 1):
                            ins = dve.scalar_tensor_tensor(out=tmp[:, u % 2, :], in0=xpad[:, u % 2, tap:tap + TB],
                                                           scalar=convp[:, cc, tap:tap + 1], in1=tmp[:, u % 2, :],
                                                           op0=ALU.mult, op1=ALU.add)
                            if tap < TAPS - 2:
                                link(ins)
                        ins.then_inc(conv_ready, 1)
                        dve.wait_ge(conv_silu, u + 1)
                        dve.tensor_tensor(h32[:], tmp[:, u % 2, :], sil[:, u % 2, :], ALU.mult).then_inc(h32_ready, 1)
                        dve.wait_ge(h_high, u + 1)
                        dve.tensor_tensor(hidden[:, u % HSLOTS, 1, 0, :], h32[:], hidden[:, u % HSLOTS, 0, 0, :],
                                          ALU.subtract).then_inc(h_ready, 1)
                    else:
                        dve.wait_ge(h_high, u + 1)
                        dve.scalar_tensor_tensor(out=hidden[:, u % HSLOTS, 1, :, :], in0=ring[:, 2 * s:2 * s + 2, :],
                                                 scalar=0.0, in1=hidden[:, u % HSLOTS, 0, :, :], op0=ALU.max,
                                                 op1=ALU.subtract).then_inc(freed, 1)
                elif kind == "evac":
                    u = step[1]
                    ph, g, b, c = units[u]
                    scale = 1 / WS if ph == MIX else 1 / WS ** 2
                    for t in range(NT):
                        dve.wait_ge(tile_done, NT * u + t + 1)
                        dve.scalar_tensor_tensor(out=acc[:, b, t, :], in0=downs[:, t, :], scalar=scale,
                                                 in1=acc[:, b, t, :], op0=ALU.mult, op1=ALU.add
                                                 ).then_inc(acc_added, 1)
                    dve.wait_ge(acc_added, NT * (u // 4 + 1))
                    if (ph, g) == (MIX, 1):
                        nat_free(1, b)
                        rms_norm(acc[:, b])
                    elif (ph, g) == (MLP, 1):
                        dve.wait_ge(x_loaded, 16 * (NB + b + 1))
                        dve.tensor_tensor(acc[:, b], acc[:, b], xin, ALU.add).then_inc(x_used, 1)
                        dve.wait_ge(x_used, NB + b + 1)
                        nat_free(2, b)
                        layer_norm(acc[:, b], nat, nat_ready)
                elif kind == "G":
                    b = step[1]
                    item = item_of[step]
                    s = item % 2
                    dve.wait_ge(filled, 2 * item + 2)
                    dve.tensor_scalar(score[:].rearrange("p (a t) e -> p a (t e)", a=2),
                                      ring[:, 2 * s:2 * s + 2, 0:2 * E], 1 / WS, None, ALU.mult).then_inc(freed, 1)
                    dve.wait_ge(freed, item + 1)
                    link(dve.tensor_reduce(small[:, 0, :], score[:], AX.X, ALU.max))
                    dve.tensor_tensor(score[:], score[:], small[:, 0, :].unsqueeze(2).to_broadcast([P, NT, E]),
                                      ALU.subtract).then_inc(exp_in, 1)
                    dve.wait_ge(exp_done, b + 1)
                    link(dve.tensor_reduce(small[:, 2, :], prob[:], AX.X, ALU.add))
                    link(dve.reciprocal(small[:, 3, :], small[:, 2, :]))
                    link(dve.tensor_tensor(prob[:], prob[:], small[:, 3, :].unsqueeze(2).to_broadcast([P, NT, E]),
                                           ALU.mult))
                    link(dve.tensor_tensor(biased[:, :, 0:E], prob[:], gbias[:].unsqueeze(1).to_broadcast([P, NT, E]),
                                           ALU.add))
                    for t in range(NT):
                        ins = dve.max(best[:, t, :], biased[:, t, :])
                    link(ins)
                    link(dve.memset(best[:, :, TOP:8], FLOOR))
                    for t in range(NT):
                        ins = dve.match_replace(marked[:, t, :], best[:, t, :], biased[:, t, :], TAKEN)
                    link(ins)
                    link(dve.tensor_tensor(cw[:], marked[:, :, 0:E], biased[:, :, 0:E], ALU.not_equal))
                    dve.tensor_tensor(cw[:], cw[:], prob[:], ALU.mult).then_inc(cw_ready, 1)
                elif kind == "W":
                    b = step[1]
                    item = item_of[step]
                    s = item % 2
                    dve.wait_ge(filled, 2 * item + 2)
                    dve.tensor_copy(cwt[0:E, :].rearrange("e (a t) -> e a t", a=2), ring[0:E, 2 * s:2 * s + 2, 0:2 * P])
                    dve.wait_ge(cw_stored, 16 * (8 + b))
                    dve.tensor_scalar(cws[:].rearrange("e (a t) -> e a t", a=2), ring[0:E, 2 * s:2 * s + 2, 0:2 * P],
                                      1 / WS, None, ALU.mult).then_inc(freed, 1)
                elif kind == "B":
                    _, b, h = step
                    item = item_of[step]
                    s = item % 2
                    dve.wait_ge(filled, 2 * item + 2)
                    dve.tensor_tensor(acc[:, b, 2 * h:2 * h + 2, :], acc[:, b, 2 * h:2 * h + 2, :],
                                      ring[:, 2 * s:2 * s + 2, :], ALU.add).then_inc(freed, 1)

            def unit_moe(m0, c0, k):
                s = k % 2
                c = k % UNITS[MOE]
                dve.wait_ge(filled, m0 * 2 + (2 * (N_ITEMS + k) + 2))
                dve.wait_ge(silu_ready, m0 + (32 + k + 1))
                dve.scalar_tensor_tensor(out=tmp[:, 0, :], in0=ring[:, 2 * s + 1, :],
                                         scalar=ebias[:, k // N_MOE % 2, c, 1:2], in1=sil[:, s, :], op0=ALU.add,
                                         op1=ALU.mult).then_inc(freed, 1)
                dve.wait_ge(freed, m0 + (N_ITEMS + k + 1))
                dve.wait_ge(cw_loaded[c], c0 * 16 + 16 * (k // UNITS[MOE] + 1))
                dve.tensor_tensor(h32[:], tmp[:, 0, :], cw_rows[:, c, :], ALU.mult).then_inc(h32_ready, 1)
                dve.wait_ge(h_high, m0 + (N_UNITS + k + 1))
                dve.tensor_tensor(hidden[:, k % HSLOTS, 1, 0, :], h32[:], hidden[:, k % HSLOTS, 0, 0, :],
                                  ALU.subtract).then_inc(h_ready, 1)

            def add_moe(m0, r0, k):
                run = k // UNITS[MOE]
                for t in range(NT):
                    dve.wait_ge(tile_done, m0 * NT + (NT * (N_UNITS + k) + t + 1))
                    dve.wait_ge(acc_added, r0 * NT + (NT * (N_RUNS + run - NB) + t + 1))
                    dve.scalar_tensor_tensor(out=acc[:, run % NB, t, :], in0=downs[:, t, :], scalar=1 / WS,
                                             in1=acc[:, run % NB, t, :], op0=ALU.mult, op1=ALU.add
                                             ).then_inc(acc_added, 1)

            def turn(i, n_splits):
                m0, r0 = i * PAIR, i * (PAIR // UNITS[MOE])
                for k in range(PAIR):
                    unit_moe(m0, r0, k)
                    if k and k % UNITS[MOE] == 0:
                        add_moe(m0, r0, k - 1)
                    j = split_slots.get(k)
                    if j is not None and j < n_splits:
                        high = i * (2 * UNITS[MOE]) + (22 + j)
                        buf, slot = (1 + j // 5) % 2, (21 + j) % 2
                        dve.wait_ge(w_high, high)
                        up_bias(slot, buf, j % 5)
                        low_part(slot, buf, j % 5 * COLS[MOE], COLS[MOE], high)
                add_moe(m0, r0, PAIR - 1)

            with dve.Fori(0, PAIRS - 1) as i:
                turn(i, 10)
            turn(PAIRS - 1, 5)


def layouts(a):
    import numpy as np

    def up(w, c0):
        rows = w[c0:c0 + P]
        return np.transpose(rows.reshape(P, KD, P), (2, 1, 0)).reshape(P, KD * P)

    w_in, w_out = a["L0_attn_W_in"], a["L0_attn_W_out"]
    w_mix = np.stack([np.concatenate([up(w_in, c * P), up(w_in, 1024 + c * P), w_out[:, c * P:(c + 1) * P].T], 1)
                      for c in range(8)])
    w1, w2 = a["L0_attn_W_mlp1"], a["L0_attn_W_mlp2"]
    w_mlp = np.stack([np.concatenate([up(w1, 2 * c * P), up(w1, (2 * c + 1) * P)]
                                     + [w2[:, r * P:(r + 1) * P].T for r in (2 * c, 2 * c + 1)], 1)
                      for c in range(8)])

    def long(shared, routed):
        rows = np.concatenate([shared, routed], 0)
        return np.concatenate([rows, np.zeros((HROWS - rows.shape[0],) + rows.shape[1:], rows.dtype)], 0)

    e1 = long(a["L0_ffn_ws1"], a["L0_ffn_w1"].reshape(E * HE, D))
    e3 = long(a["L0_ffn_ws3"], a["L0_ffn_w3"].reshape(E * HE, D))
    e2 = long(a["L0_ffn_ws2"].T, np.transpose(a["L0_ffn_w2"], (0, 2, 1)).reshape(E * HE, D))
    b1 = long(a["L0_ffn_bs1"], a["L0_ffn_b1"].reshape(-1))
    b3 = long(a["L0_ffn_bs3"], a["L0_ffn_b3"].reshape(-1))
    w_moe = np.stack([np.concatenate([up(e1, r), up(e3, r), e2[r:r + P], b1[r:r + P, None], b3[r:r + P, None]], 1)
                      for r in range(0, HROWS, P)])
    conv = np.concatenate([a["L0_attn_conv_w"][:, 0, :], a["L0_attn_conv_b"][:, None]], 1)
    conv = np.transpose(conv.reshape(8, P, TAPS + 1), (1, 0, 2))
    gate_w = np.transpose(a["L0_ffn_gate_w"].reshape(E, KD, P), (2, 1, 0))
    out_bias = np.concatenate([a["L0_ffn_b2"], a["L0_ffn_bs2"][None]], 0)
    return {"x": a["L0_attn_x"].reshape(T, D), "w_mix": w_mix, "w_mlp": w_mlp, "w_moe": w_moe, "conv": conv,
            "gate_w": gate_w, "gate_b": a["L0_ffn_gate_b"], "out_bias": out_bias}


def kernel(**inputs):
    import numpy as np
    import concourse.bacc as bacc
    from concourse.bass_utils import run_bass_kernel_spmd

    arrays = {n: np.ascontiguousarray(v) for n, v in layouts({n: np.asarray(v) for n, v in inputs.items()}).items()}
    nc = bacc.Bacc("TRN2", target_bir_lowering=False, num_devices=1)
    args = [nc.dram_tensor(n, v.shape, F32, kind="ExternalInput").ap() for n, v in arrays.items()]
    args.append(nc.dram_tensor("out", (T, D), F32, kind="ExternalOutput").ap())
    layer(nc, *args)
    got = run_bass_kernel_spmd(nc, [arrays], core_ids=[0])
    return got.results[0]["out"].reshape(NB, TB, D)
```

```python
from contextlib import ExitStack

import concourse.bass as bass
from concourse import mybir

F32 = mybir.dt.float32
F16 = mybir.dt.float16
I32 = mybir.dt.int32
U32 = mybir.dt.uint32
ALU = mybir.AluOpType
ACT = mybir.ActivationFunctionType
AX = mybir.AxisListType

P = 128
D = 512
KD = D // P
T = 2048
NB = 4
TB = T // NB
NT = TB // P
TAPS = 4
E = 16
TOP = 6
HE = 352
SHARED = 2
NTS = 3
SLOT = NTS * P
MAX_SLOTS = -(-T // SLOT)
N_SLOTS = (TOP * T + E * (SLOT - 1)) // SLOT
PER = 3
SHARED_UNITS = (3, 3)
WS = 64.0
EPS = 1e-5
FLOOR = -3.0e38
TAKEN = -3.3e38
MIX, MLP, SHARED = range(3)

UP = 2 * KD * P
COLS = {MIX: UP + D, MLP: UP + 2 * D, SHARED: UP + D}
WCOLS = 4 * COLS[MLP]
XG = WCOLS - KD * SLOT
PASSES = ((0, 0), (0, 1), (1, 0))
HSLOTS = 3
ROWBUFS = 8


def plan():
    per = {(MIX, 0): 4, (MIX, 1): 4, (MLP, 0): 4, (MLP, 1): 4, (SHARED, 0): SHARED_UNITS[0],
           (SHARED, 1): SHARED_UNITS[1]}
    units = [(ph, g, b, c, c == n - 1) for (ph, g), n in per.items() for b in range(NB) for c in range(n)]
    at = {u[:4]: n for n, u in enumerate(units)}
    ahead = at[SHARED, 1, 0, 0]
    after = {n: [] for n in range(ahead + 2)}
    for b in range(NB - 1):
        after[at[MIX, 0, b, 0]].append(("prep", b + 1))
        after[at[MIX, 0, b, 2]] += [("T", 0, b + 1, h) for h in range(2)]
    for b in range(NB):
        nxt = (MIX, 1, b + 1, 2) if b + 1 < NB else (MLP, 0, 0, 2)
        after[at[nxt]] += [("T", 1, b, h) for h in range(2)]
        first = at[MLP, 1, b, 2] + 4
        after[first] += [("T", 2, b, h) for h in range(2)]
        after[first + 1].append(("G", b))
        after[first + 2].append(("P", b))
        after[first + 3] += [("W", b)] + [("B", b, h) for h in range(2)]
    for group in range(3):
        for j in range(4):
            after[16 * group + 3 * j + 3].append(("split", 4 * (group + 1) + j))
    for j, u in enumerate((51, 54, 57)):
        after[u].append(("split", 16 + j))
    after[ahead - 3].append(("rows",))
    first = 16 + SHARED_UNITS[0]
    for n, u in enumerate((ahead - 4, ahead - 3, ahead - 2, ahead, ahead + 1, ahead + 1)):
        after[u].append(("split", first + n))

    def down(n):
        return [("D", n), ("evac", n)] if units[n][4] else [("D", n)]

    steps = [("prep", 0)] + [("split", w) for w in range(4)] + [("T", 0, 0, 0), ("T", 0, 0, 1)]
    for n in range(ahead):
        steps += (down(n - 2) if n >= 2 else []) + [("U", n)] + after[n]
    steps += [("RT", 0, 0)] + down(ahead - 2) + [("RT", 0, 1), ("RU", 0)] + after[ahead]
    steps += down(ahead - 1) + [("RU", 1)] + after[ahead + 1]

    r = PER * (N_SLOTS - 1)
    tail = [("RD", r), ("RU", r + 2), ("RD", r + 1), ("U", ahead), ("RD", r + 2),
            ("Revac", N_SLOTS - 1), ("U", ahead + 1)]
    gathered = 0
    for n in range(ahead + 2, len(units)):
        tail += down(n - 2) + [("U", n)]
        if n >= ahead + 4:
            tail += [("C", gathered + j) for j in range(6)]
            gathered += 6
    tail += down(len(units) - 2) + down(len(units) - 1)
    tail += [("C", n) for n in range(gathered, TOP * T // P)]
    return units, ahead, steps, tail


def layer(nc, x, w_mix, w_mlp, w_shared, w_moe, conv, gate_w, gate_b, out_bias, out):
    units, N_AHEAD, steps, tail = plan()
    items = [s for s in steps if s[0] in ("T", "U", "G", "P", "W", "B", "RT", "RU")]
    item_of = {s: n for n, s in enumerate(items)}
    N_ITEMS = len(items)
    SLOT_ITEMS = 2 + PER
    N_LOOP = N_SLOTS - 1
    tail_items = [s for s in tail if s[0] in ("U", "RU")]
    item_of.update({s: N_ITEMS + SLOT_ITEMS * N_LOOP + n for n, s in enumerate(tail_items)})
    N_SPLITS = 16 + SHARED_UNITS[0]
    R_UNITS = PER * N_SLOTS
    run_of, run = {}, 0
    for n, unit in enumerate(units):
        run_of[n] = run
        run += unit[4]
        if n + 1 == N_AHEAD:
            N_RUNS = run
            run += N_SLOTS
    assert N_LOOP % 2 == 0 and 2 * PER % HSLOTS == 0 and max(SHARED_UNITS) <= PER

    def seq(u):
        return u if u < N_AHEAD else u + R_UNITS

    def gated(u):
        return u if units[u][0] == MIX else seq(u) - 32

    R0 = N_AHEAD - 32

    f_rows = nc.dram_tensor("f_rows", [T, D], F32, kind="Internal").ap()
    y_rows = nc.dram_tensor("y_rows", [N_SLOTS * SLOT, D], F32, kind="Internal").ap()
    token_at = nc.dram_tensor("token_at", [E * T, 1], I32, kind="Internal").ap()
    slot_dram = nc.dram_tensor("slot_dram", [P, 2], I32, kind="Internal").ap()

    with ExitStack() as ctx:
        def sb(name, shape, dt=F32):
            return ctx.enter_context(nc.sbuf_tensor(name, shape, dt))

        def sem(name):
            return ctx.enter_context(nc.semaphore(name))

        weights = sb("weights", [P, 2, 2, WCOLS], F16)
        xt = sb("xt", [P, NB, 2, KD, TB], F16)
        acc = sb("acc", [P, NB, NT, D])
        staged = sb("staged", [P, 2, COLS[MLP]])
        hidden = sb("hidden", [P, HSLOTS, 2, 2, TB], F16)
        rows = sb("rows", [P, 2, NT, D])
        xin, nat = rows[:, 0], rows[:, 1]
        got = rows[:].rearrange("p a t d -> p (a t) d")
        yout = sb("yout", [P, NTS, D])
        tmp = sb("tmp", [P, 2, TB])
        sil = sb("sil", [P, 2, TB])
        h32 = sb("h32", [P, TB])
        xpad = sb("xpad", [P, 2, TAPS - 1 + TB + 1])
        ident = sb("ident", [P, P])
        convp = sb("convp", [P, 8, TAPS + 1])
        stats = sb("stats", [P, NT, 6])
        mv = sb("mv", [P, NT, 2])
        small = sb("small", [P, 4, NT])
        gate32 = sb("gate32", [P, KD, E])
        gate16 = sb("gate16", [P, 2, KD, E], F16)
        gbias = sb("gbias", [P, E])
        score = sb("score", [P, NT, E])
        prob = sb("prob", [P, NT, E])
        biased = sb("biased", [P, NT, E + 2])
        marked = sb("marked", [P, NT, E + 2])
        best = sb("best", [P, NT, 8])
        cw = sb("cw", [P, NT, E])
        cwt = sb("cwt", [E + 1, TB])
        ob = sb("ob", [E + 1, D])
        ebias = sb("ebias", [P, 2, 4, 2])
        ones16 = sb("ones16", [P, P], F16)
        before16 = sb("before16", [P, P], F16)
        mask = sb("mask", [P, NT, E])
        mask16 = sb("mask16", [P, NT, E], F16)
        prior16 = sb("prior16", [P, NT + 1, E], F16)
        place = sb("place", [P, NT, E])
        first_place = sb("first_place", [P, E])
        expert_no = sb("expert_no", [P, E])
        rank = sb("rank", [P, 2, NT, E])
        pick = sb("pick", [P, 2, NT, E])
        place_k = sb("place_k", [P, NB, NT, TOP])
        weight_k = sb("weight_k", [P, NB, NT, TOP])
        place_i = sb("place_i", [P, NT, TOP], I32)
        out_i = sb("out_i", [P, NB, NT, TOP], I32)
        expert_f = sb("expert_f", [P, NT * TOP])
        shift = sb("shift", [P, E])
        low_i = sb("low_i", [P, NT, TOP], I32)
        high_i = sb("high_i", [P, NT, TOP], I32)
        table_i = sb("table_i", [P, NB, NT, TOP], I32)
        token_no = sb("token_no", [P, NB * NT], I32)
        count = sb("count", [P, E])
        slots_of = sb("slots_of", [P, E])
        upto = sb("upto", [P, 2, E])
        slot_no = sb("slot_no", [P, 1])
        slot_f = sb("slot_f", [P, 4])
        slot_i = sb("slot_i", [P, 2], I32)
        slot_row = sb("slot_row", [1, 2 * P], I32)
        tokens = sb("tokens", [P, E * T // P + MAX_SLOTS * NTS - T // P], I32)
        tokens_now = sb("tokens_now", [P, 2, NTS], I32)

        ring = ctx.enter_context(nc.psum_tensor("ring", [P, 4, TB], F32))
        downs = ctx.enter_context(nc.psum_tensor("downs", [P, NT, D], F32))

        w_loaded = [sem(f"w_loaded{i}") for i in range(2)]
        rows_loaded = [sem(f"rows_loaded{i}") for i in range(2)]
        got_loaded = [sem(f"got_loaded{i}") for i in range(ROWBUFS)]
        x_loaded = sem("x_loaded")
        const_loaded = sem("const_loaded")
        stored = sem("stored")
        table_set = sem("table_set")
        slot_stored = sem("slot_stored")
        slot_loaded = sem("slot_loaded")
        tokens_loaded = sem("tokens_loaded")
        out_stored = sem("out_stored")
        ident_ready = sem("ident_ready")
        pool_step = sem("pool_step")
        gathering = sem("gathering")
        now_ready = sem("now_ready")
        filled = sem("filled")
        tile_done = sem("tile_done")
        w_high = sem("w_high")
        sqrt_done = sem("sqrt_done")
        exp_done = sem("exp_done")
        gate_high = sem("gate_high")
        t_high = sem("t_high")
        xp_ready = sem("xp_ready")
        silu_ready = sem("silu_ready")
        conv_silu = sem("conv_silu")
        h_high = sem("h_high")
        w_ready = sem("w_ready")
        freed = sem("freed")
        sqrt_in = sem("sqrt_in")
        exp_in = sem("exp_in")
        x_used = sem("x_used")
        nat_ready = sem("nat_ready")
        mask_ready = sem("mask_ready")
        gate_ready = sem("gate_ready")
        cw_ready = sem("cw_ready")
        conv_ready = sem("conv_ready")
        places_ready = sem("places_ready")
        slots_ready = sem("slots_ready")
        got_used = sem("got_used")
        h32_ready = sem("h32_ready")
        h_ready = sem("h_ready")
        acc_added = sem("acc_added")
        dve_step = sem("dve_step")

        def split_place(w):
            if w < 16:
                ph = (MIX, MLP)[w // 8]
                return w // 4 % 2, w % 4, COLS[ph]
            if w < N_SPLITS:
                return 0, w - 16, COLS[SHARED]
            n = w - N_SPLITS
            if n >= PER * N_SLOTS:
                return (N_SLOTS + 1) % 2, n - PER * N_SLOTS, COLS[SHARED]
            return (n // PER + 1) % 2, n % PER, COLS[SHARED]

        def split_after(w):
            if w < 16:
                return tiles(16 * max(0, w // 4 - 1))
            if w < N_SPLITS:
                return tiles(48)
            n = w - N_SPLITS
            if n < PER:
                return tiles(64)
            if n < 2 * PER:
                return tiles(N_AHEAD - SHARED_UNITS[0] + n - PER + 1)
            return tiles(N_AHEAD + n - 2 * PER + 1)

        def tiles(n):
            routed = min(max(n - N_AHEAD, 0), R_UNITS)
            return NT * (n - routed) + NTS * routed

        def sums(run):
            routed = min(max(run - N_RUNS, 0), N_SLOTS)
            return NT * (run - routed) + NTS * routed

        def t_item(n, b, h):
            return item_of[("T", n, b, h)]

        def unit_weights(u):
            ph, g, _, c, _ = units[u]
            return (0 if ph == SHARED else g), c * COLS[ph]

        block = ctx.enter_context(nc.Block())

        @block.sync
        def _(sp):
            def load_x(b):
                sp.dma_start(xin, x[b * TB:(b + 1) * TB, :].rearrange("(t p) d -> p t d", p=P)).then_inc(x_loaded, 16)

            def load_w(w, source):
                if w >= 2:
                    sp.wait_ge(w_ready, w - 1)
                sp.dma_start(staged[:, w % 2, 0:source.shape[-1]], source).then_inc(w_loaded[w % 2], 16)

            load_x(0)
            for dst, src in ((convp[:], conv), (gate32[:], gate_w), (gbias[:], gate_b.partition_broadcast(P)),
                             (ob[:], out_bias)):
                sp.dma_start(dst, src).then_inc(const_loaded, 16)
            x_after = {3: 1, 4: 2, 5: 3, 10: 4, 17: 5}

            def store_f(b):
                sp.wait_ge(nat_ready, 2 * NB + b + 1)
                sp.dma_start(f_rows[b * TB:(b + 1) * TB, :].rearrange("(t p) d -> p t d", p=P), nat
                             ).then_inc(stored, 16)

            for w in range(N_SPLITS):
                load_w(w, w_mix[w] if w < 8 else w_mlp[w - 8] if w < 16 else w_shared[w - 16])
                if w in x_after:
                    n = x_after[w]
                    sp.wait_ge(x_used, n)
                    load_x(n % NB)
            for b in range(NB):
                store_f(b)
                if b < 2:
                    sp.wait_ge(x_used, NB + 2 + b)
                    load_x(2 + b)
            sp.wait_ge(slots_ready, 1)
            sp.dma_start(slot_dram, slot_i[:]).then_inc(slot_stored, 16)
            sp.wait_ge(slot_stored, 16)
            sp.dma_start(slot_row[:], slot_dram.rearrange("(a s) q -> a (s q)", a=1)).then_inc(slot_loaded, 16)
            sp.wait_ge(slot_loaded, 16)

            def load_slot(s, par):
                unit = sp.value_load(slot_row[0:1, bass.ds(s * 2 + 1, 1)], min_val=0, max_val=PER * (E - 1))
                for c in range(PER):
                    n = par * PER + c
                    sp.wait_ge(w_ready, s * PER + (N_SPLITS + c - 1))
                    place_now = (N_SPLITS + n) % 2
                    sp.dma_start(staged[:, place_now, 0:COLS[SHARED] + 2],
                                 w_moe[bass.ds(unit + c, 1), :, :].rearrange("a p n -> (a p) n")
                                 ).then_inc(w_loaded[place_now], 16)

            def store_slot(s):
                sp.wait_ge(acc_added, s * NTS + (NT * N_RUNS + NTS))
                dst = y_rows.rearrange("(q p) d -> p q d", p=P)[:, bass.ds(s * NTS, NTS), :]
                sp.dma_start(dst, yout[:]).then_inc(stored, 16)

            late = 2
            for i in range(late):
                load_slot(i, i % 2)
            with sp.Fori(0, N_SLOTS - 1 - late, 2) as j:
                for i in range(2):
                    load_slot(j + (late + i), i)
                    store_slot(j + i)
            load_slot(N_SLOTS - 1, 0)
            for i in range(max(SHARED_UNITS[1], late + 1)):
                if i < SHARED_UNITS[1]:
                    load_w(N_SPLITS + R_UNITS + i, w_shared[SHARED_UNITS[0] + i])
                if i < late + 1:
                    store_slot(N_SLOTS - 1 - late + i)
            for b in range(NB):
                for t in range(NT):
                    sp.wait_ge(acc_added, sums(N_RUNS + N_SLOTS + b) + t + 1)
                    sp.wait_ge(got_used, TOP * (b * NT + t + 1))
                    r = b * TB + t * P
                    sp.dma_start(out[r:r + P, :], acc[:, b, t, :]).then_inc(out_stored, 16)
            sp.wait_ge(out_stored, 16 * NB * NT)

        @block.gpsimd
        def _(pool):
            pool.memset(ident[:], 0.0).then_inc(pool_step, 1)
            pool.wait_ge(pool_step, 1)
            pool.affine_select(out=ident[:], in_=ident[:], compare_op=ALU.not_equal, fill=1.0, base=0,
                               pattern=[[-1, P]], channel_multiplier=1).then_inc(ident_ready, 1)
            pool.memset(ones16[:], 1.0).then_inc(pool_step, 1)
            pool.wait_ge(pool_step, 2)
            pool.affine_select(out=before16[:], in_=ones16[:], compare_op=ALU.is_gt, fill=0.0, base=0,
                               pattern=[[1, P]], channel_multiplier=-1).then_inc(pool_step, 1)
            pool.iota(token_no[:], pattern=[[P, NB * NT]], base=0, channel_multiplier=1).then_inc(pool_step, 1)
            pool.iota(first_place[:], pattern=[[T, E]], base=0, channel_multiplier=0,
                      allow_small_or_imprecise_dtypes=True).then_inc(pool_step, 1)
            pool.iota(expert_no[:], pattern=[[1, E]], base=0, channel_multiplier=0,
                      allow_small_or_imprecise_dtypes=True).then_inc(pool_step, 1)
            pool.iota(slot_no[:], pattern=[[0, 1]], base=0, channel_multiplier=1,
                      allow_small_or_imprecise_dtypes=True).then_inc(pool_step, 1)
            pool.memset(tokens[:], 0).then_inc(pool_step, 1)
            pool.wait_ge(pool_step, 8)
            pool.dma_start(token_at.rearrange("(p q) a -> p (q a)", p=P), tokens[:, 0:E * T // P]).then_inc(table_set, 16)
            pool.wait_ge(table_set, 16)
            for b in range(NB):
                pool.wait_ge(places_ready, b + 1)
                for t in range(NT):
                    for k in range(TOP):
                        pool.indirect_dma_start(
                            token_at, bass.IndirectOffsetOnAxis(ap=table_i[:, b, t, k:k + 1].bitcast(U32), axis=0),
                            token_no[:, b * NT + t:b * NT + t + 1], None).then_inc(table_set, 16)
            pool.wait_ge(table_set, 16 * (1 + NB * NT * TOP))
            pool.dma_start(tokens[:, 0:E * T // P], token_at.rearrange("(p q) a -> p (q a)", p=P)).then_inc(tokens_loaded, 16)
            pool.wait_ge(tokens_loaded, 16)
            pool.wait_ge(slot_loaded, 16)

            def gather(s, par):
                column = pool.value_load(slot_row[0:1, bass.ds(s * 2, 1)], min_val=0, max_val=(E - 1) * (T // P) + (MAX_SLOTS - 1) * NTS)
                pool.tensor_copy(tokens_now[:, par, :], tokens[:, bass.ds(column, NTS)]).then_inc(now_ready, 1)
                pool.wait_ge(stored, 16 * NB)
                pool.wait_ge(now_ready, s + 1)
                pool.sem_inc(gathering, 1)
                for t in range(NTS):
                    pool.indirect_dma_start(
                        rows[:, par, t, :], None, f_rows,
                        bass.IndirectOffsetOnAxis(ap=tokens_now[:, par, t:t + 1].bitcast(U32), axis=0)
                        ).then_inc(rows_loaded[par], 16)

            pool.wait_ge(freed, t_item(2, NB - 1, 1) + 1)
            gather(0, 0)
            gather(1, 1)
            with pool.Fori(0, N_SLOTS - 3, 2) as j:
                for par in range(2):
                    pool.wait_ge(filled, j * (2 * SLOT_ITEMS) + (2 * (N_ITEMS + SLOT_ITEMS * (par - 1) + 2) + 2))
                    gather(j + (2 + par), par)
            pool.wait_ge(filled, 2 * (N_ITEMS + SLOT_ITEMS * (N_SLOTS - 4) + 2) + 2)
            gather(N_SLOTS - 1, 0)
            pool.wait_ge(stored, 16 * (NB + N_SLOTS))
            for n in range(NB * NT * TOP):
                b, t, k = n // (NT * TOP), n // TOP % NT, n % TOP
                if n >= ROWBUFS:
                    pool.wait_ge(got_used, n - ROWBUFS + 1)
                pool.indirect_dma_start(
                    got[:, n % ROWBUFS, :], None, y_rows,
                    bass.IndirectOffsetOnAxis(ap=out_i[:, b, t, k:k + 1].bitcast(U32), axis=0)
                    ).then_inc(got_loaded[n % ROWBUFS], 16)

        @block.tensor
        def _(pe):
            def up(slot, buf, base, rows_t, n_tok=TB):
                for m in range(2):
                    for k in range(KD):
                        w0 = base + (m * KD + k) * P
                        for n, (pw, px) in enumerate(PASSES):
                            mm = pe.matmul(ring[:, 2 * slot + m, 0:n_tok], weights[:, buf, pw, w0:w0 + P], rows_t(px, k),
                                           start=(k == 0 and n == 0), stop=(k == KD - 1 and n == 2))
                    mm.then_inc(filled, 1)

            def down(hslot, chunks, buf, base, first, last, read, n_tiles=NT):
                for t in range(n_tiles):
                    if first and read is not None:
                        pe.wait_ge(acc_added, read[t])
                    for c in range(chunks):
                        w0 = base + UP + c * D
                        for n, (ph, pw) in enumerate(PASSES):
                            mm = pe.matmul(downs[:, t, :], hidden[:, hslot, ph, c, t * P:(t + 1) * P],
                                           weights[:, buf, pw, w0:w0 + D], start=(first and c == 0 and n == 0),
                                           stop=(last and c == chunks - 1 and n == 2))
                    mm.then_inc(tile_done, 1)

            def slot_for(item):
                if item >= 2:
                    pe.wait_ge(freed, item - 1)
                return item % 2

            def transpose_rows(slot, source, h, n_tiles=NT):
                for k in range(2):
                    for t in range(n_tiles):
                        d0 = (2 * h + k) * P
                        tr = pe.transpose(ring[:, 2 * slot + k, t * P:(t + 1) * P], source[:, t, d0:d0 + P], ident[:])
                    tr.then_inc(filled, 1)

            def up_unit(step):
                u = step[1]
                ph, g, b, c, _ = units[u]
                s = slot_for(item_of[step])
                if g == 0 and c == 0:
                    pe.wait_ge(freed, t_item(ph, b, 1) + 1)
                if b == 0:
                    if ph != SHARED:
                        pe.wait_ge(w_ready, 8 * ph + 4 * g + c + 1)
                    elif g == 0:
                        pe.wait_ge(w_ready, 16 + c + 1)
                    else:
                        pe.wait_ge(w_ready, N_SPLITS + R_UNITS + c + 1)
                up(s, *unit_weights(u), lambda px, k: xt[:, b, px, k, :])

            def sums_read(run):
                return [min(sums(run - 1) + t + 1, sums(run)) for t in range(NT)]

            def down_unit(u):
                ph, g, b, c, last = units[u]
                if ph == MLP:
                    pe.wait_ge(freed, item_of[("U", u)] + 1)
                else:
                    pe.wait_ge(h_ready, gated(u) + 1)
                down(seq(u) % HSLOTS, 1 + (ph == MLP), *unit_weights(u), c == 0, last,
                     sums_read(run_of[u]) if run_of[u] else None)

            def transpose_slot(t, l, h):
                item = t * (2 * SLOT_ITEMS) + (N_ITEMS + SLOT_ITEMS * l + h)
                pe.wait_ge(freed, item - 1)
                par = (l + 1) % 2
                pe.wait_ge(rows_loaded[par], t * (16 * NTS) + 16 * NTS * ((l + 1) // 2 + 1))
                transpose_rows((N_ITEMS + SLOT_ITEMS * l + h) % 2, rows[:, par], h, NTS)

            def up_slot(t, item, n):
                pe.wait_ge(freed, t * (2 * SLOT_ITEMS) + (item - 1))
                pe.wait_ge(w_ready, t * (2 * PER) + (N_SPLITS + n + 1))
                buf = (n // PER + 1) % 2
                up(item % 2, buf, n % PER * COLS[SHARED],
                   lambda px, k: weights[:, buf, px, XG + k * SLOT:XG + (k + 1) * SLOT], SLOT)

            def down_slot(t, n):
                pe.wait_ge(h_ready, t * (2 * PER) + (R0 + n + 1))
                c = n % PER
                down((N_AHEAD + n) % HSLOTS, 1, (n // PER + 1) % 2, c * COLS[SHARED], c == 0, c == PER - 1,
                     [t * (2 * NTS) + (NT * N_RUNS + NTS * (n // PER - 1) + k + 1) for k in range(NTS)], NTS)

            def walk(order):
                for step in order:
                    kind = step[0]
                    if kind == "T":
                        _, n, b, h = step
                        s = slot_for(item_of[step])
                        pe.wait_ge(nat_ready, NB * n + b + 1)
                        transpose_rows(s, nat, h)
                    elif kind == "U":
                        up_unit(step)
                    elif kind == "D":
                        down_unit(step[1])
                    elif kind == "G":
                        b = step[1]
                        s = slot_for(item_of[step])
                        pe.wait_ge(freed, t_item(2, b, 1) + 1)
                        pe.wait_ge(gate_ready, 1)
                        for t in range(NT):
                            for k in range(KD):
                                for n, (px, pw) in enumerate(PASSES):
                                    mm = pe.matmul(ring[:, 2 * s + t // 2, t % 2 * E:(t % 2 + 1) * E],
                                                   xt[:, b, px, k, t * P:(t + 1) * P], gate16[:, pw, k, :],
                                                   start=(k == 0 and n == 0), stop=(k == KD - 1 and n == 2))
                            if t % 2:
                                mm.then_inc(filled, 1)
                    elif kind == "P":
                        s = slot_for(item_of[step])
                        pe.wait_ge(mask_ready, step[1] + 1)
                        pe.matmul(ring[:, 2 * s, 0:NT * E], before16[:], mask16[:].rearrange("p t e -> p (t e)"),
                                  start=True, stop=False)
                        pe.matmul(ring[:, 2 * s, 0:NT * E], ones16[:],
                                  prior16[:, 0:NT, :].rearrange("p t e -> p (t e)"),
                                  start=False, stop=True).then_inc(filled, 1)
                        pe.matmul(ring[:, 2 * s + 1, 0:E], ones16[:], prior16[:, NT, :],
                                  start=True, stop=True).then_inc(filled, 1)
                    elif kind == "W":
                        s = slot_for(item_of[step])
                        pe.wait_ge(cw_ready, step[1] + 1)
                        for t in range(NT):
                            tr = pe.transpose(ring[0:E, 2 * s + t // 2, t % 2 * P:(t % 2 + 1) * P], cw[:, t, :],
                                              ident[:])
                            if t % 2:
                                tr.then_inc(filled, 1)
                    elif kind == "B":
                        _, b, h = step
                        s = slot_for(item_of[step])
                        pe.wait_ge(freed, item_of[("W", b)] + 1)
                        pe.wait_ge(const_loaded, 64)
                        for t in range(2):
                            t0 = (2 * h + t) * P
                            pe.matmul(ring[:, 2 * s + t, :], cwt[:, t0:t0 + P], ob[:],
                                      start=True, stop=True).then_inc(filled, 1)
                    elif kind == "RT":
                        s = slot_for(item_of[step])
                        pe.wait_ge(rows_loaded[0], 16 * NTS)
                        transpose_rows(s, rows[:, 0], step[2], NTS)
                    elif kind == "RU":
                        if step[1] == 0:
                            pe.wait_ge(freed, item_of[("RT", 0, 1)] + 1)
                        up_slot(0 if step[1] < 2 else N_LOOP // 2,
                                item_of[step] if step[1] < 2 else N_ITEMS, step[1] % (2 * PER))
                    elif kind == "RD":
                        down_slot(N_LOOP // 2, step[1] % (2 * PER))

            pe.wait_ge(ident_ready, 1)
            pe.wait_ge(pool_step, 8)
            walk(steps)
            with pe.Fori(0, N_LOOP // 2) as t:
                for l in range(2):
                    i, n = N_ITEMS + SLOT_ITEMS * l, PER * l
                    transpose_slot(t, l, 0)
                    down_slot(t, n)
                    transpose_slot(t, l, 1)
                    up_slot(t, i + 2, n + 2)
                    down_slot(t, n + 1)
                    up_slot(t, i + 3, n + 3)
                    down_slot(t, n + 2)
                    up_slot(t, i + 4, n + 4)
            walk(tail)

        @block.scalar
        def _(act):
            roots = 0
            exps = 0

            def root():
                nonlocal roots
                roots += 1
                act.wait_ge(sqrt_in, roots)
                act.activation(small[:, 1, :], small[:, 0, :], ACT.Sqrt).then_inc(sqrt_done, 1)

            def split_high(stage, loads, free_at, buf, base, cols):
                act.wait_ge(w_loaded[stage], loads)
                if free_at is not None:
                    act.wait_ge(tile_done, free_at)
                act.activation(weights[:, buf, 0, base:base + cols], staged[:, stage, 0:cols], ACT.Copy,
                               scale=WS).then_inc(w_high, 1)

            def gated_unit(fill, slot, silu_slot, bias, read, hslot, done, n_tok=TB):
                act.wait_ge(filled, fill)
                act.activation(sil[:, silu_slot, 0:n_tok], ring[:, 2 * slot, 0:n_tok], ACT.Silu, scale=1 / WS,
                               bias=bias).then_inc(silu_ready, 1)
                act.wait_ge(freed, read)
                act.wait_ge(tile_done, done)
                act.activation(hidden[:, hslot, 0, 0, 0:n_tok], tmp[:, silu_slot, 0:n_tok], ACT.Copy,
                               scale=1 / WS).then_inc(h_high, 1)

            def transposed_slot(t, l, h):
                c0 = N_ITEMS + SLOT_ITEMS * l + h
                act.wait_ge(filled, t * (4 * SLOT_ITEMS) + (2 * c0 + 2))
                x0 = XG + 2 * h * SLOT
                act.activation(weights[:, l % 2, 0, x0:x0 + 2 * SLOT].rearrange("p (k t) -> p k t", k=2),
                               ring[:, 2 * (c0 % 2):2 * (c0 % 2) + 2, 0:SLOT], ACT.Copy).then_inc(t_high, 1)

            def unit_slot(t, item, n):
                gated_unit(t * (4 * SLOT_ITEMS) + (2 * item + 1), item % 2, (R0 + n) % 2,
                           ebias[:, (n // PER + 1) % 2, n % PER, 0:1],
                           t * (2 * SLOT_ITEMS) + (item + 1), (N_AHEAD + n) % HSLOTS,
                           t * (2 * PER * NTS) + tiles(N_AHEAD + n - HSLOTS + 1), SLOT)

            def split_slot(t, n):
                w = N_SPLITS + n
                split_high(w % 2, t * (PER * 16) + 16 * (w // 2 + 1),
                           t * (2 * PER * NTS) + tiles(N_AHEAD + n - 2 * PER + 1), (n // PER + 1) % 2,
                           n % PER * COLS[SHARED], COLS[SHARED])

            def copy_slot(t, l):
                act.wait_ge(stored, t * 32 + 16 * (NB + l))
                for k in range(NTS):
                    act.wait_ge(tile_done, t * (2 * PER * NTS) + (tiles(N_AHEAD + PER * l + 2) + k + 1))
                    act.activation(yout[:, k, :], downs[:, k, :], ACT.Copy, scale=1 / WS).then_inc(acc_added, 1)

            def walk(order):
                nonlocal exps
                for step in order:
                    kind = step[0]
                    if kind == "split":
                        w = step[1]
                        buf, j, cols = split_place(w)
                        split_high(w % 2, 16 * (w // 2 + 1), split_after(w) or None, buf, j * cols, cols)
                    elif kind == "prep":
                        root()
                        root()
                    elif kind == "T":
                        _, n, b, h = step
                        s = item_of[step] % 2
                        act.wait_ge(filled, 2 * item_of[step] + 2)
                        act.activation(xt[:, b, 0, 2 * h:2 * h + 2, :], ring[:, 2 * s:2 * s + 2, :],
                                       ACT.Copy).then_inc(t_high, 1)
                    elif kind == "U":
                        u = step[1]
                        ph, g, b, c, _ = units[u]
                        item = item_of[step]
                        s = item % 2
                        if ph == MIX:
                            act.wait_ge(filled, 2 * item + 1)
                            if u >= 2:
                                act.wait_ge(conv_ready, u - 1)
                            act.activation(xpad[:, u % 2, TAPS - 1:TAPS - 1 + TB], ring[:, 2 * s, :], ACT.Copy,
                                           scale=1 / WS).then_inc(xp_ready, 1)
                            act.wait_ge(filled, 2 * item + 2)
                            if u >= 2:
                                act.wait_ge(h32_ready, u - 1)
                            act.activation(sil[:, u % 2, :], ring[:, 2 * s + 1, :], ACT.Silu,
                                           scale=1 / WS).then_inc(silu_ready, 1)
                            act.wait_ge(conv_ready, u + 1)
                            act.activation(tmp[:, u % 2, :], tmp[:, u % 2, :], ACT.Silu).then_inc(conv_silu, 1)
                            act.wait_ge(h32_ready, u + 1)
                            if u >= HSLOTS:
                                act.wait_ge(tile_done, tiles(u - HSLOTS + 1))
                            act.activation(hidden[:, u % HSLOTS, 0, 0, :], h32[:], ACT.Copy).then_inc(h_high, 1)
                        elif ph == MLP:
                            act.wait_ge(filled, 2 * item + 2)
                            act.wait_ge(tile_done, tiles(u - HSLOTS + 1))
                            act.activation(hidden[:, u % HSLOTS, 0, :, :], ring[:, 2 * s:2 * s + 2, :],
                                           ACT.Relu).then_inc(h_high, 1)
                        else:
                            gated_unit(2 * item + 1, s, gated(u) % 2, ebias[:, 0, c, 0:1], item + 1,
                                       seq(u) % HSLOTS, tiles(seq(u) - HSLOTS + 1))
                    elif kind == "evac" and units[step[1]][:2] in ((MIX, 1), (MLP, 1)):
                        root()
                    elif kind == "G":
                        exps += 1
                        act.wait_ge(exp_in, exps)
                        act.activation(prob[:], score[:], ACT.Exp).then_inc(exp_done, 1)
                    elif kind == "RT":
                        transposed_first(item_of[step], step[2])
                    elif kind == "RU":
                        if step[1] < 2:
                            unit_slot(0, item_of[step], step[1])
                        else:
                            unit_slot(N_LOOP // 2, N_ITEMS, step[1] % (2 * PER))
                    elif kind == "Revac":
                        copy_slot(N_LOOP // 2, 0)

            def transposed_first(item, h):
                act.wait_ge(filled, 2 * item + 2)
                x0 = XG + 2 * h * SLOT
                act.activation(weights[:, 1, 0, x0:x0 + 2 * SLOT].rearrange("p (k t) -> p k t", k=2),
                               ring[:, 2 * (item % 2):2 * (item % 2) + 2, 0:SLOT], ACT.Copy).then_inc(t_high, 1)

            act.wait_ge(const_loaded, 64)
            act.activation(gate16[:, 0], gate32[:], ACT.Copy, scale=WS).then_inc(gate_high, 1)
            walk(steps)
            with act.Fori(0, N_LOOP // 2) as t:
                for l in range(2):
                    i, n = N_ITEMS + SLOT_ITEMS * l, PER * l
                    transposed_slot(t, l, 0)
                    transposed_slot(t, l, 1)
                    split_slot(t, n + 6)
                    unit_slot(t, i + 2, n + 2)
                    split_slot(t, n + 7)
                    unit_slot(t, i + 3, n + 3)
                    copy_slot(t, l)
                    split_slot(t, n + 8)
                    unit_slot(t, i + 4, n + 4)
            walk(tail)

        @block.vector
        def _(dve):
            steps_done = 0
            roots = 0

            def link(ins):
                nonlocal steps_done
                steps_done += 1
                ins.then_inc(dve_step, 1)
                dve.wait_ge(dve_step, steps_done)

            def root():
                nonlocal roots
                roots += 1
                dve.wait_ge(sqrt_done, roots)

            def split_low(stage, buf, base, cols, high, bias):
                dve.wait_ge(w_high, high)
                if bias is not None:
                    dve.tensor_copy(bias[:, 0:1], staged[:, stage, cols:cols + 1])
                    dve.tensor_scalar(bias[:, 1:2], staged[:, stage, cols + 1:cols + 2], WS, None, ALU.mult)
                dve.scalar_tensor_tensor(out=weights[:, buf, 1, base:base + cols], in0=staged[:, stage, 0:cols],
                                         scalar=WS, in1=weights[:, buf, 0, base:base + cols], op0=ALU.mult,
                                         op1=ALU.subtract).then_inc(w_ready, 1)

            def nat_free(n, b):
                if n or b:
                    before = (n, b - 1) if b else (n - 1, NB - 1)
                    dve.wait_ge(filled, 2 * t_item(*before, 1) + 2)
                if n == 2 and b:
                    dve.wait_ge(stored, 16 * b)

            def layer_norm(src, dst, ends):
                for t in range(NT):
                    ins = dve.bn_stats(stats[:, t, :], src[:, t, :])
                link(ins)
                for t in range(NT):
                    ins = dve.bn_aggr(mv[:, t, :], stats[:, t, :])
                link(ins)
                dve.tensor_scalar(small[:, 0, :], mv[:, :, 1], EPS, None, ALU.add).then_inc(sqrt_in, 1)
                root()
                link(dve.reciprocal(small[:, 2, :], small[:, 1, :]))
                for t in range(NT):
                    ins = dve.tensor_scalar(dst[:, t, :], src[:, t, :], mv[:, t, 0:1], small[:, 2, t:t + 1],
                                            ALU.subtract, ALU.mult)
                ins.then_inc(ends, 1)

            def rms_norm(src):
                for t in range(NT):
                    ins = dve.tensor_tensor_reduce(nat[:, t, :], src[:, t, :], src[:, t, :], 1.0, 0.0, ALU.mult,
                                                   ALU.add, small[:, 0, t:t + 1])
                ins.then_inc(sqrt_in, 1)
                root()
                link(dve.tensor_scalar(small[:, 2, :], small[:, 1, :], 1e-12, None, ALU.max))
                link(dve.reciprocal(small[:, 3, :], small[:, 2, :]))
                for t in range(NT):
                    ins = dve.tensor_scalar(nat[:, t, :], src[:, t, :], small[:, 3, t:t + 1], float(D) ** 0.5,
                                            ALU.mult, ALU.mult)
                ins.then_inc(nat_ready, 1)

            def mixer_unit(u, item):
                cc = 4 * units[u][1] + units[u][3]
                dve.wait_ge(xp_ready, u + 1)
                dve.wait_ge(silu_ready, u + 1)
                dve.tensor_scalar(tmp[:, u % 2, :], xpad[:, u % 2, TAPS - 1:TAPS - 1 + TB],
                                  convp[:, cc, TAPS - 1:TAPS], convp[:, cc, TAPS:TAPS + 1], ALU.mult,
                                  ALU.add).then_inc(freed, 1)
                dve.wait_ge(freed, item + 1)
                for tap in range(TAPS - 1):
                    ins = dve.scalar_tensor_tensor(out=tmp[:, u % 2, :], in0=xpad[:, u % 2, tap:tap + TB],
                                                   scalar=convp[:, cc, tap:tap + 1], in1=tmp[:, u % 2, :],
                                                   op0=ALU.mult, op1=ALU.add)
                    if tap < TAPS - 2:
                        link(ins)
                ins.then_inc(conv_ready, 1)
                dve.wait_ge(conv_silu, u + 1)
                dve.tensor_tensor(h32[:], tmp[:, u % 2, :], sil[:, u % 2, :], ALU.mult).then_inc(h32_ready, 1)
                dve.wait_ge(h_high, u + 1)
                dve.tensor_tensor(hidden[:, u % HSLOTS, 1, 0, :], h32[:], hidden[:, u % HSLOTS, 0, 0, :],
                                  ALU.subtract).then_inc(h_ready, 1)

            def gated_unit(fill, slot, silu_at, silu_slot, bias, hslot, high, n_tok=TB):
                dve.wait_ge(filled, fill)
                dve.wait_ge(silu_ready, silu_at)
                dve.scalar_tensor_tensor(out=tmp[:, silu_slot, 0:n_tok], in0=ring[:, 2 * slot + 1, 0:n_tok],
                                         scalar=bias, in1=sil[:, silu_slot, 0:n_tok], op0=ALU.add, op1=ALU.mult).then_inc(freed, 1)
                dve.wait_ge(h_high, high)
                dve.scalar_tensor_tensor(out=hidden[:, hslot, 1, 0, 0:n_tok], in0=tmp[:, silu_slot, 0:n_tok],
                                         scalar=1 / WS, in1=hidden[:, hslot, 0, 0, 0:n_tok], op0=ALU.mult,
                                         op1=ALU.subtract).then_inc(h_ready, 1)

            def gate(b, item):
                s = item % 2
                dve.wait_ge(filled, 2 * item + 2)
                dve.tensor_scalar(score[:].rearrange("p (a t) e -> p a (t e)", a=2),
                                  ring[:, 2 * s:2 * s + 2, 0:2 * E], 1 / WS, None, ALU.mult).then_inc(freed, 1)
                dve.wait_ge(freed, item + 1)
                link(dve.tensor_reduce(small[:, 0, :], score[:], AX.X, ALU.max))
                dve.tensor_tensor(score[:], score[:], small[:, 0, :].unsqueeze(2).to_broadcast([P, NT, E]),
                                  ALU.subtract).then_inc(exp_in, 1)
                dve.wait_ge(exp_done, b + 1)
                link(dve.tensor_reduce(small[:, 2, :], prob[:], AX.X, ALU.add))
                link(dve.reciprocal(small[:, 3, :], small[:, 2, :]))
                link(dve.tensor_tensor(prob[:], prob[:], small[:, 3, :].unsqueeze(2).to_broadcast([P, NT, E]),
                                       ALU.mult))
                link(dve.tensor_tensor(biased[:, :, 0:E], prob[:], gbias[:].unsqueeze(1).to_broadcast([P, NT, E]),
                                       ALU.add))
                for t in range(NT):
                    ins = dve.max(best[:, t, :], biased[:, t, :])
                link(ins)
                link(dve.memset(best[:, :, TOP:8], FLOOR))
                for t in range(NT):
                    ins = dve.match_replace(marked[:, t, :], best[:, t, :], biased[:, t, :], TAKEN)
                link(ins)
                link(dve.tensor_tensor(mask[:], marked[:, :, 0:E], biased[:, :, 0:E], ALU.not_equal))
                dve.tensor_tensor(cw[:], mask[:], prob[:], ALU.mult).then_inc(cw_ready, 1)
                if b:
                    dve.wait_ge(filled, 2 * item_of[("P", b - 1)] + 2)
                    link(dve.tensor_copy(prior16[:, 0, :], prior16[:, NT, :]))
                dve.tensor_copy(mask16[:], mask[:])
                for t in range(NT):
                    ins = dve.tensor_tensor(prior16[:, t + 1, :], prior16[:, t, :], mask[:, t, :], ALU.add)
                    if t + 1 < NT:
                        link(ins)
                ins.then_inc(mask_ready, 1)

            def running_sum(src, bufs):
                step = 1
                for n in range(4):
                    dst = bufs[n % 2]
                    dve.tensor_copy(dst[..., 0:step], src[..., 0:step])
                    link(dve.tensor_tensor(dst[..., step:E], src[..., step:E], src[..., 0:E - step], ALU.add))
                    src, step = dst, 2 * step
                return src

            def places(b, item):
                s = item % 2
                dve.wait_ge(filled, 2 * item + 2)
                if b == NB - 1:
                    dve.tensor_copy(count[:], ring[:, 2 * s + 1, 0:E])
                dve.tensor_tensor(place[:], ring[:, 2 * s, 0:NT * E].rearrange("p (t e) -> p t e", t=NT),
                                  first_place[:].unsqueeze(1).to_broadcast([P, NT, E]), ALU.add).then_inc(freed, 1)
                dve.wait_ge(freed, item + 1)
                if b == NB - 1:
                    slot_table()
                upto_here = running_sum(mask[:], (rank[:, 0], rank[:, 1]))
                dve.wait_ge(cw_ready, b + 1)
                link(dve.tensor_tensor(rank[:, 0], upto_here, mask[:], ALU.mult))
                for k in range(TOP):
                    for a, src in enumerate((place, cw)):
                        ins = dve.scalar_tensor_tensor(out=pick[:, a], in0=rank[:, 0], scalar=float(k + 1), in1=src[:],
                                                       op0=ALU.is_equal, op1=ALU.mult)
                    link(ins)
                    dve.tensor_reduce(place_k[:, b, :, k], pick[:, 0], AX.X, ALU.add)
                    link(dve.tensor_reduce(weight_k[:, b, :, k], pick[:, 1], AX.X, ALU.add))
                link(dve.tensor_copy(place_i[:], place_k[:, b]))
                dve.tensor_scalar(low_i[:], place_i[:], P - 1, None, ALU.bitwise_and)
                link(dve.tensor_scalar(high_i[:], place_i[:], 7, None, ALU.logical_shift_right))
                dve.scalar_tensor_tensor(out=table_i[:, b], in0=low_i[:], scalar=float(E * T // P), in1=high_i[:],
                                         op0=ALU.mult, op1=ALU.add).then_inc(places_ready, 1)

            def slot_table():
                link(dve.tensor_scalar(slots_of[:], count[:], 0.0, None, ALU.is_gt))
                for j in range(1, MAX_SLOTS):
                    link(dve.scalar_tensor_tensor(out=slots_of[:], in0=count[:], scalar=float(SLOT * j),
                                                  in1=slots_of[:], op0=ALU.is_gt, op1=ALU.add))
                total = running_sum(slots_of[:], (upto[:, 0], upto[:, 1]))
                link(dve.tensor_scalar(pick[:, 0, 0, :], total, slot_no[:, 0:1], None, ALU.is_le))
                link(dve.tensor_reduce(slot_f[:, 0:1], pick[:, 0, 0, :], AX.X, ALU.add))
                link(dve.tensor_scalar(slot_f[:, 0:1], slot_f[:, 0:1], float(E - 1), None, ALU.min))
                link(dve.tensor_tensor(pick[:, 0, 1, :], total, slots_of[:], ALU.subtract))
                dve.scalar_tensor_tensor(out=shift[:], in0=pick[:, 0, 1, :], scalar=float(SLOT), in1=first_place[:],
                                         op0=ALU.mult, op1=ALU.subtract)
                link(dve.scalar_tensor_tensor(out=pick[:, 0, 2, :], in0=expert_no[:], scalar=slot_f[:, 0:1],
                                              in1=pick[:, 0, 1, :], op0=ALU.is_equal, op1=ALU.mult))
                link(dve.tensor_reduce(slot_f[:, 1:2], pick[:, 0, 2, :], AX.X, ALU.add))
                link(dve.tensor_tensor(slot_f[:, 2:3], slot_no[:], slot_f[:, 1:2], ALU.subtract))
                link(dve.tensor_scalar(slot_f[:, 2:3], slot_f[:, 2:3], float(MAX_SLOTS - 1), float(NTS), ALU.min,
                                       ALU.mult))
                link(dve.scalar_tensor_tensor(out=slot_f[:, 3:4], in0=slot_f[:, 0:1], scalar=float(T // P),
                                              in1=slot_f[:, 2:3], op0=ALU.mult, op1=ALU.add))
                dve.tensor_copy(slot_i[:, 0:1], slot_f[:, 3:4])
                dve.tensor_scalar(slot_i[:, 1:2], slot_f[:, 0:1], float(PER), None, ALU.mult).then_inc(slots_ready, 1)

            def out_rows():
                eq = h32[:, 0:NT * TOP * E].rearrange("p (n e) -> p n e", e=E)
                for b in range(NB):
                    link(dve.tensor_copy(place_i[:], place_k[:, b]))
                    link(dve.tensor_scalar(low_i[:], place_i[:], T.bit_length() - 1, None, ALU.logical_shift_right))
                    link(dve.tensor_copy(expert_f[:], low_i[:].rearrange("p t k -> p (t k)")))
                    link(dve.tensor_tensor(eq, expert_f[:].unsqueeze(2).to_broadcast([P, NT * TOP, E]),
                                           expert_no[:].unsqueeze(1).to_broadcast([P, NT * TOP, E]), ALU.is_equal))
                    link(dve.tensor_tensor(eq, eq, shift[:].unsqueeze(1).to_broadcast([P, NT * TOP, E]), ALU.mult))
                    link(dve.tensor_reduce(expert_f[:], eq, AX.X, ALU.add))
                    link(dve.tensor_tensor(out_i[:, b].rearrange("p t k -> p (t k)"), expert_f[:],
                                           place_k[:, b].rearrange("p t k -> p (t k)"), ALU.add))

            def transposed_low(item, s, high, buf, h):
                dve.wait_ge(t_high, high)
                x0 = XG + 2 * h * SLOT
                parts = [weights[:, buf, p, x0:x0 + 2 * SLOT].rearrange("p (k t) -> p k t", k=2) for p in range(2)]
                dve.tensor_tensor(parts[1], ring[:, 2 * s:2 * s + 2, 0:SLOT], parts[0], ALU.subtract).then_inc(freed, 1)

            def unit_slot(t, item, n):
                gated_unit(t * (4 * SLOT_ITEMS) + (2 * item + 2), item % 2, t * (2 * PER) + (R0 + n + 1), (R0 + n) % 2,
                           ebias[:, (n // PER + 1) % 2, n % PER, 1:2], (N_AHEAD + n) % HSLOTS,
                           t * (2 * PER) + (N_AHEAD + n + 1), SLOT)

            def split_slot(t, n):
                w = N_SPLITS + n
                buf = (n // PER + 1) % 2
                split_low(w % 2, buf, n % PER * COLS[SHARED], COLS[SHARED], t * (2 * PER) + (w + 1),
                          ebias[:, buf, n % PER])

            def walk(order):
                adds = [0]
                for step in order:
                    kind = step[0]
                    if kind == "split":
                        w = step[1]
                        buf, j, cols = split_place(w)
                        split_low(w % 2, buf, j * cols, cols, w + 1, ebias[:, buf, j] if w >= 16 else None)
                    elif kind == "prep":
                        b = step[1]
                        dve.wait_ge(x_loaded, 16 * (b + 1))
                        layer_norm(xin, acc[:, b], x_used)
                        dve.wait_ge(x_used, b + 1)
                        nat_free(0, b)
                        rms_norm(acc[:, b])
                    elif kind == "T":
                        _, n, b, h = step
                        s = item_of[step] % 2
                        dve.wait_ge(t_high, 2 * (NB * n + b) + h + 1)
                        dve.tensor_tensor(xt[:, b, 1, 2 * h:2 * h + 2, :], ring[:, 2 * s:2 * s + 2, :],
                                          xt[:, b, 0, 2 * h:2 * h + 2, :], ALU.subtract).then_inc(freed, 1)
                    elif kind == "U":
                        u = step[1]
                        ph, g, b, c, _ = units[u]
                        item = item_of[step]
                        s = item % 2
                        if ph == MIX:
                            mixer_unit(u, item)
                        elif ph == MLP:
                            dve.wait_ge(h_high, u + 1)
                            dve.scalar_tensor_tensor(out=hidden[:, u % HSLOTS, 1, :, :],
                                                     in0=ring[:, 2 * s:2 * s + 2, :], scalar=0.0,
                                                     in1=hidden[:, u % HSLOTS, 0, :, :], op0=ALU.max,
                                                     op1=ALU.subtract).then_inc(freed, 1)
                        else:
                            gated_unit(2 * item + 2, s, gated(u) + 1, gated(u) % 2, ebias[:, 0, c, 1:2],
                                       seq(u) % HSLOTS, seq(u) + 1)
                    elif kind == "evac":
                        u = step[1]
                        ph, g, b, c, _ = units[u]
                        scale = 1 / WS ** 2 if ph == MLP else 1 / WS
                        if adds[0]:
                            dve.wait_ge(got_used, adds[0])
                        for t in range(NT):
                            dve.wait_ge(tile_done, tiles(seq(u)) + t + 1)
                            dve.scalar_tensor_tensor(out=acc[:, b, t, :], in0=downs[:, t, :], scalar=scale,
                                                     in1=acc[:, b, t, :], op0=ALU.mult, op1=ALU.add
                                                     ).then_inc(acc_added, 1)
                        dve.wait_ge(acc_added, sums(run_of[u] + 1))
                        if (ph, g) == (MIX, 1):
                            nat_free(1, b)
                            rms_norm(acc[:, b])
                        elif (ph, g) == (MLP, 1):
                            dve.wait_ge(x_loaded, 16 * (NB + b + 1))
                            dve.tensor_tensor(acc[:, b], acc[:, b], xin, ALU.add).then_inc(x_used, 1)
                            dve.wait_ge(x_used, NB + b + 1)
                            nat_free(2, b)
                            layer_norm(acc[:, b], nat, nat_ready)
                    elif kind == "G":
                        gate(step[1], item_of[step])
                    elif kind == "P":
                        places(step[1], item_of[step])
                    elif kind == "rows":
                        out_rows()
                    elif kind == "W":
                        b = step[1]
                        item = item_of[step]
                        s = item % 2
                        dve.wait_ge(filled, 2 * item + 2)
                        dve.tensor_copy(cwt[0:E, :].rearrange("e (a t) -> e a t", a=2),
                                        ring[0:E, 2 * s:2 * s + 2, 0:2 * P]).then_inc(freed, 1)
                    elif kind == "B":
                        _, b, h = step
                        item = item_of[step]
                        s = item % 2
                        dve.wait_ge(filled, 2 * item + 2)
                        dve.tensor_tensor(acc[:, b, 2 * h:2 * h + 2, :], acc[:, b, 2 * h:2 * h + 2, :],
                                          ring[:, 2 * s:2 * s + 2, :], ALU.add).then_inc(freed, 1)
                    elif kind == "RT":
                        item = item_of[step]
                        transposed_low(item, item % 2, 24 + step[2] + 1, 1, step[2])
                    elif kind == "RU":
                        if step[1] < 2:
                            unit_slot(0, item_of[step], step[1])
                        else:
                            unit_slot(N_LOOP // 2, N_ITEMS, step[1] % (2 * PER))
                    elif kind == "C":
                        n = step[1]
                        b, t, k = n // (NT * TOP), n // TOP % NT, n % TOP
                        dve.wait_ge(got_loaded[n % ROWBUFS], 16 * (n // ROWBUFS + 1))
                        if n:
                            dve.wait_ge(got_used, n)
                        dve.scalar_tensor_tensor(out=acc[:, b, t, :], in0=got[:, n % ROWBUFS, :],
                                                 scalar=weight_k[:, b, t, k:k + 1], in1=acc[:, b, t, :], op0=ALU.mult,
                                                 op1=ALU.add).then_inc(got_used, 1)
                        adds[0] = n + 1

            dve.memset(xpad[:], 0.0)
            dve.memset(biased[:], FLOOR)
            dve.memset(prior16[:], 0.0)
            link(dve.memset(cwt[:], 1.0))
            dve.wait_ge(pool_step, 8)
            dve.wait_ge(gate_high, 1)
            dve.scalar_tensor_tensor(out=gate16[:, 1], in0=gate32[:], scalar=WS, in1=gate16[:, 0], op0=ALU.mult,
                                     op1=ALU.subtract).then_inc(gate_ready, 1)
            walk(steps)
            with dve.Fori(0, N_LOOP // 2) as t:
                for l in range(2):
                    i, n = N_ITEMS + SLOT_ITEMS * l, PER * l
                    for h in range(2):
                        transposed_low(None, (i + h) % 2, t * 4 + (24 + 2 * (l + 1) + h + 1), l % 2, h)
                    split_slot(t, n + 6)
                    unit_slot(t, i + 2, n + 2)
                    split_slot(t, n + 7)
                    unit_slot(t, i + 3, n + 3)
                    split_slot(t, n + 8)
                    unit_slot(t, i + 4, n + 4)
            walk(tail)


def layouts(a):
    import numpy as np

    def up(w, c0):
        rows = w[c0:c0 + P]
        return np.transpose(rows.reshape(P, KD, P), (2, 1, 0)).reshape(P, KD * P)

    w_in, w_out = a["L0_attn_W_in"], a["L0_attn_W_out"]
    w_mix = np.stack([np.concatenate([up(w_in, c * P), up(w_in, 1024 + c * P), w_out[:, c * P:(c + 1) * P].T], 1)
                      for c in range(8)])
    w1, w2 = a["L0_attn_W_mlp1"], a["L0_attn_W_mlp2"]
    w_mlp = np.stack([np.concatenate([up(w1, 2 * c * P), up(w1, (2 * c + 1) * P)]
                                     + [w2[:, r * P:(r + 1) * P].T for r in (2 * c, 2 * c + 1)], 1)
                      for c in range(8)])

    def expert_units(u1, u3, u2, c1, c3):
        fill = -u1.shape[0] % P
        u1, u3, u2, c1, c3 = (np.concatenate([v, np.zeros((fill,) + v.shape[1:], v.dtype)], 0)
                              for v in (u1, u3, u2, c1, c3))
        return np.stack([np.concatenate([up(u1, r), up(u3, r), u2[r:r + P], c1[r:r + P, None], c3[r:r + P, None]], 1)
                         for r in range(0, u1.shape[0], P)])

    w_shared = expert_units(a["L0_ffn_ws1"], a["L0_ffn_ws3"], a["L0_ffn_ws2"].T, a["L0_ffn_bs1"], a["L0_ffn_bs3"])
    w_moe = np.concatenate([expert_units(a["L0_ffn_w1"][e], a["L0_ffn_w3"][e], a["L0_ffn_w2"][e].T, a["L0_ffn_b1"][e],
                                         a["L0_ffn_b3"][e]) for e in range(E)], 0)
    conv = np.concatenate([a["L0_attn_conv_w"][:, 0, :], a["L0_attn_conv_b"][:, None]], 1)
    conv = np.transpose(conv.reshape(8, P, TAPS + 1), (1, 0, 2))
    gate_w = np.transpose(a["L0_ffn_gate_w"].reshape(E, KD, P), (2, 1, 0))
    out_bias = np.concatenate([a["L0_ffn_b2"], a["L0_ffn_bs2"][None]], 0)
    return {"x": a["L0_attn_x"].reshape(T, D), "w_mix": w_mix, "w_mlp": w_mlp, "w_shared": w_shared, "w_moe": w_moe, "conv": conv,
            "gate_w": gate_w, "gate_b": a["L0_ffn_gate_b"], "out_bias": out_bias}


def kernel(**inputs):
    import numpy as np
    import concourse.bacc as bacc
    from concourse.bass_utils import run_bass_kernel_spmd

    arrays = {n: np.ascontiguousarray(v) for n, v in layouts({n: np.asarray(v) for n, v in inputs.items()}).items()}
    nc = bacc.Bacc("TRN2", target_bir_lowering=False, num_devices=1)
    args = [nc.dram_tensor(n, v.shape, F32, kind="ExternalInput").ap() for n, v in arrays.items()]
    args.append(nc.dram_tensor("out", (T, D), F32, kind="ExternalOutput").ap())
    layer(nc, *args)
    got = run_bass_kernel_spmd(nc, [arrays], core_ids=[0])
    return got.results[0]["out"].reshape(NB, TB, D)
```

```python
from contextlib import ExitStack

import concourse.bass as bass
from concourse import mybir

F32 = mybir.dt.float32
F16 = mybir.dt.float16
I32 = mybir.dt.int32
U32 = mybir.dt.uint32
ALU = mybir.AluOpType
ACT = mybir.ActivationFunctionType
AX = mybir.AxisListType

P = 128
D = 512
KD = D // P
T = 2048
NB = 4
TB = T // NB
NT = TB // P
TAPS = 4
E = 16
TOP = 6
HE = 352
SHARED = 2
NTS = 3
SLOT = NTS * P
MAX_SLOTS = -(-T // SLOT)
N_SLOTS = (TOP * T + E * (SLOT - 1)) // SLOT
PER = 3
SHARED_UNITS = (3, 3)
WS = 64.0
EPS = 1e-5
FLOOR = -3.0e38
TAKEN = -3.3e38
MIX, MLP, SHARED = range(3)

UP = 2 * KD * P
COLS = {MIX: UP + D, MLP: UP + 2 * D, SHARED: UP + D}
WCOLS = 4 * COLS[MLP]
XG = WCOLS - KD * SLOT
PASSES = ((0, 0), (0, 1), (1, 0))
HSLOTS = 3
BIAS_AT = (0, 32, 64)
BIAS_ROWS = 96
ROWBUFS = 8
FIRST_SLOTS = [min(N_SLOTS, (TOP * T + (E - TOP + k + 1) * (SLOT - 1)) // SLOT) for k in range(TOP)]
EARLY_FROM = FIRST_SLOTS[0] + 1
EARLY_ADDS = 2
TAIL_ADDS = 7


def plan():
    per = {(MIX, 0): 4, (MIX, 1): 4, (MLP, 0): 4, (MLP, 1): 4, (SHARED, 0): SHARED_UNITS[0],
           (SHARED, 1): SHARED_UNITS[1]}
    units = [(ph, g, b, c, c == n - 1) for (ph, g), n in per.items() for b in range(NB) for c in range(n)]
    at = {u[:4]: n for n, u in enumerate(units)}
    ahead = at[SHARED, 1, 0, 0]
    before, after = ({n: [] for n in range(ahead + 2)} for _ in range(2))
    before[0] += [("T", 0, 0, 0), ("T", 0, 0, 1), ("split", 1), ("stats", 1)]
    after[0] += [("split", 2), ("center", 1)]
    after[1] += [("squares", 0, 1), ("scale", 0, 1), ("split", 3)]
    before[3].append(("T", 0, 1, 0))
    after[2].append(("stats", 2))
    after[3] += [("T", 0, 1, 1), ("center", 2), ("squares", 0, 2)]
    after[4].append(("scale", 0, 2))
    after[5].append(("stats", 3))
    after[6].append(("center", 3))
    after[7].append(("squares", 0, 3))
    after[8].append(("scale", 0, 3))
    for b in range(2, NB):
        u = at[MIX, 0, b, 0]
        before[u - 2].append(("T", 0, b, 0))
        before[u - 1].append(("T", 0, b, 1))
    for b in range(NB):
        last = at[MIX, 1, b, 3]
        after[last + 2].append(("squares", 1, b))
        after[last + 2].append(("scale", 1, b))
        before[last + 5].append(("T", 1, b, 0))
        before[last + 6].append(("T", 1, b, 1))
        after[at[MLP, 0, b, 1]].append(("X", b))
        last = at[MLP, 1, b, 3]
        before[last + 2].insert(0, ("final", b))
        for n, step in enumerate((("T", 2, b, 0), ("T", 2, b, 1), ("G", b), ("P", b))):
            before[last + 3 + n].append(step)
        after[last + 6].append(("places", b))
        after[at[MLP, 1, NB - 1, 3] + 8 + b].append(("rows", b))
    after[at[MLP, 1, NB - 1, 3] + 7].append(("slots",))
    for group in range(3):
        for j in range(4):
            after[16 * group + 3 * j + 3].append(("split", 4 * (group + 1) + j))
    for j, u in enumerate((51, 54, 57)):
        after[u].append(("split", 16 + j))
    first = 16 + SHARED_UNITS[0]
    for n, u in enumerate((ahead - 4, ahead - 3, ahead - 2, ahead - 1)):
        after[u].append(("split", first + n))

    def down(n):
        return [("D", n), ("evac", n)] if units[n][4] else [("D", n)]

    steps = [("stats", 0), ("center", 0), ("squares", 0, 0), ("scale", 0, 0), ("split", 0)]
    for n in range(ahead):
        steps += (down(n - 2) if n >= 2 else []) + before[n] + [("U", n)] + after[n]
    steps += [("RT", 0, 0)] + down(ahead - 2) + [("RT", 0, 1), ("split", first + 4), ("RU", 0)]
    steps += down(ahead - 1) + [("split", first + 5), ("RU", 1)]

    r = PER * (N_SLOTS - 1)
    tail = [("RD", r), ("RU", r + 2), "adds", ("RD", r + 1), ("U", ahead), "adds", ("RD", r + 2),
            ("Revac", N_SLOTS - 1), ("U", ahead + 1), "adds"]
    for n in range(ahead + 2, len(units)):
        tail += down(n - 2) + [("U", n), "adds"]
    tail += down(len(units) - 2) + ["adds"] + down(len(units) - 1)
    places = [i for i, step in enumerate(tail) if step == "adds"]
    first, total = EARLY_ADDS * PER * (N_SLOTS - 1 - EARLY_FROM), TOP * T // P
    for n, i in reversed(list(enumerate(places))):
        tail[i:i + 1] = [("C", m) for m in range(first + TAIL_ADDS * n, min(first + TAIL_ADDS * (n + 1), total))]
    assert first + TAIL_ADDS * len(places) >= total
    return units, ahead, steps, tail


def layer(nc, x, w_mix, w_mlp, w_shared, w_moe, conv, gate_w, gate_b, out_bias, out):
    units, N_AHEAD, steps, tail = plan()
    items = [s for s in steps if s[0] in ("T", "U", "G", "P", "RT", "RU")]
    item_of = {s: n for n, s in enumerate(items)}
    LEAD = 2
    N_ITEMS = len(items)
    SLOT_ITEMS = 2 + PER
    N_LOOP = N_SLOTS - 1
    tail_items = [s for s in tail if s[0] in ("U", "RU")]
    item_of.update({s: N_ITEMS + SLOT_ITEMS * N_LOOP + n for n, s in enumerate(tail_items)})
    N_SPLITS = 16 + SHARED_UNITS[0]
    R_UNITS = PER * N_SLOTS
    run_of, run = {}, 0
    for n, unit in enumerate(units):
        run_of[n] = run
        run += unit[4]
        if n + 1 == N_AHEAD:
            N_RUNS = run
            run += N_SLOTS
    assert N_LOOP % 2 == 0 and 2 * PER % HSLOTS == 0 and max(SHARED_UNITS) <= PER

    N_MIX, N_MLP = (sum(unit[0] == kind for unit in units) for kind in (MIX, MLP))

    def seq(u):
        return u if u < N_AHEAD else u + R_UNITS

    def gated(u):
        return u if units[u][0] == MIX else seq(u) - N_MLP

    R0 = N_AHEAD - N_MLP

    f_rows = nc.dram_tensor("f_rows", [T, D], F32, kind="Internal").ap()
    y_rows = nc.dram_tensor("y_rows", [N_SLOTS * SLOT, D], F32, kind="Internal").ap()
    token_at = nc.dram_tensor("token_at", [E * T, 1], I32, kind="Internal").ap()
    slot_dram = nc.dram_tensor("slot_dram", [P, 2], I32, kind="Internal").ap()

    with ExitStack() as ctx:
        def sb(name, shape, dt=F32):
            return ctx.enter_context(nc.sbuf_tensor(name, shape, dt))

        def sem(name):
            return ctx.enter_context(nc.semaphore(name))

        weights = sb("weights", [P, 2, 2, WCOLS], F16)
        xt = sb("xt", [P, NB, 2, KD, TB], F16)
        acc = sb("acc", [P, NB, NT, D])
        staged = sb("staged", [P, 2, COLS[MLP]])
        hidden = sb("hidden", [P, HSLOTS, 2, 2, TB], F16)
        rows = sb("rows", [P, 2, NT, D])
        xin, nat = rows[:, 0], rows[:, 1]
        yout = sb("yout", [P, NTS, D])
        tmp = sb("tmp", [P, 2, TB])
        sil = sb("sil", [P, 2, TB])
        h32 = sb("h32", [P, TB])
        xpad = sb("xpad", [P, 2, TAPS - 1 + TB + 1])
        ident = sb("ident", [P, P])
        convp = sb("convp", [P, 8, TAPS + 1])
        stats = sb("stats", [P, NT, 6])
        mv = sb("mv", [P, NT, 2])
        small = sb("small", [P, 6, NT])
        gate32 = sb("gate32", [P, KD, E])
        gate16 = sb("gate16", [P, 2, KD, E], F16)
        gbias = sb("gbias", [P, E])
        score = sb("score", [P, NT, E])
        prob = sb("prob", [P, NT, E])
        biased = sb("biased", [P, NT, E + 2])
        marked = sb("marked", [P, NT, E + 2])
        best = sb("best", [P, NT, 8])
        cw = sb("cw", [P, NT, E])
        cw16 = sb("cw16", [P, NT, BIAS_ROWS], F16)
        ob = sb("ob", [BIAS_ROWS, D])
        ob16 = sb("ob16", [BIAS_ROWS, D], F16)
        ident16 = sb("ident16", [P, P], F16)
        ebias = sb("ebias", [P, 2, 4, 2])
        ones16 = sb("ones16", [P, P], F16)
        before16 = sb("before16", [P, P], F16)
        mask = sb("mask", [P, NT, E])
        mask16 = sb("mask16", [P, NT, E], F16)
        prior16 = sb("prior16", [P, NT + 1, E], F16)
        place = sb("place", [P, NT, E])
        first_place = sb("first_place", [P, E])
        expert_no = sb("expert_no", [P, E])
        rank = sb("rank", [P, 2, NT, E])
        pick = sb("pick", [P, 2, NT, E])
        place_k = sb("place_k", [P, NB, NT, TOP])
        weight_k = sb("weight_k", [P, NB, NT, TOP])
        place_i = sb("place_i", [P, NT, TOP], I32)
        out_i = sb("out_i", [P, NB, NT, TOP], I32)
        expert_f = sb("expert_f", [P, NT * TOP])
        shift = sb("shift", [P, E])
        low_i = sb("low_i", [P, NT, TOP], I32)
        high_i = sb("high_i", [P, NT, TOP], I32)
        table_i = sb("table_i", [P, NB, NT, TOP], I32)
        token_no = sb("token_no", [P, NB * NT], I32)
        count = sb("count", [P, E])
        slots_of = sb("slots_of", [P, E])
        upto = sb("upto", [P, 2, E])
        slot_no = sb("slot_no", [P, 1])
        slot_f = sb("slot_f", [P, 4])
        slot_i = sb("slot_i", [P, 2], I32)
        slot_row = sb("slot_row", [1, 2 * P], I32)
        tokens = sb("tokens", [P, E * T // P + MAX_SLOTS * NTS - T // P], I32)
        tokens_now = sb("tokens_now", [P, 2, NTS], I32)

        ring = ctx.enter_context(nc.psum_tensor("ring", [P, 4, TB], F32))
        downs = ctx.enter_context(nc.psum_tensor("downs", [P, NT, D], F32))

        w_loaded = [sem(f"w_loaded{i}") for i in range(2)]
        rows_loaded = [sem(f"rows_loaded{i}") for i in range(2)]
        got_loaded = [sem(f"got_loaded{i}") for i in range(ROWBUFS)]
        x_loaded = sem("x_loaded")
        const_loaded = sem("const_loaded")
        stored = sem("stored")
        table_set = sem("table_set")
        slot_stored = sem("slot_stored")
        slot_loaded = sem("slot_loaded")
        tokens_loaded = sem("tokens_loaded")
        out_stored = sem("out_stored")
        ident_ready = sem("ident_ready")
        pool_step = sem("pool_step")
        gathering = sem("gathering")
        now_ready = sem("now_ready")
        filled = sem("filled")
        tile_done = sem("tile_done")
        w_high = sem("w_high")
        sqrt_done = sem("sqrt_done")
        exp_done = sem("exp_done")
        x_used = sem("x_used")
        final_ready = sem("final_ready")
        gate_high = sem("gate_high")
        t_high = sem("t_high")
        xp_ready = sem("xp_ready")
        silu_ready = sem("silu_ready")
        conv_silu = sem("conv_silu")
        h_high = sem("h_high")
        w_ready = sem("w_ready")
        freed = sem("freed")
        sqrt_in = sem("sqrt_in")
        exp_in = sem("exp_in")
        x_added = sem("x_added")
        center_ready = sem("center_ready")
        const_scaled = sem("const_scaled")
        nat_ready = sem("nat_ready")
        mask_ready = sem("mask_ready")
        gate_ready = sem("gate_ready")
        cw_ready = sem("cw_ready")
        conv_ready = sem("conv_ready")
        places_ready = sem("places_ready")
        slots_ready = sem("slots_ready")
        got_used = sem("got_used")
        h_ready = sem("h_ready")
        acc_added = sem("acc_added")
        dve_step = sem("dve_step")

        def got(n):
            c0 = PER * COLS[SHARED] + n % 2 * 2 * D
            return weights[:, n % ROWBUFS // 4, n // 2 % 2, c0:c0 + 2 * D].bitcast(F32)

        def cwt(b):
            c0 = PER * COLS[SHARED] + b % 2 * TB
            return weights[0:BIAS_ROWS, 0, b // 2, c0:c0 + TB]

        def got_tile(n):
            return n // (NB * NT), n // NT % NB, n % NT

        def split_place(w):
            if w < 16:
                ph = (MIX, MLP)[w // 8]
                return w // 4 % 2, w % 4, COLS[ph]
            if w < N_SPLITS:
                return 0, w - 16, COLS[SHARED]
            n = w - N_SPLITS
            if n >= PER * N_SLOTS:
                return (N_SLOTS + 1) % 2, n - PER * N_SLOTS, COLS[SHARED]
            return (n // PER + 1) % 2, n % PER, COLS[SHARED]

        def split_after(w):
            if w < 16:
                return tiles(16 * max(0, w // 4 - 1))
            if w < N_SPLITS:
                return tiles(48)
            n = w - N_SPLITS
            if n < PER:
                return tiles(64)
            if n < 2 * PER:
                return tiles(N_AHEAD - SHARED_UNITS[0] + n - PER + 1)
            return tiles(N_AHEAD + n - 2 * PER + 1)

        def tiles(n):
            routed = min(max(n - N_AHEAD, 0), R_UNITS)
            return NT * (n - routed) + NTS * routed

        def sums(run):
            routed = min(max(run - N_RUNS, 0), N_SLOTS)
            return NT * (run - routed) + NTS * routed

        def t_item(n, b, h):
            return item_of[("T", n, b, h)]

        def unit_weights(u):
            ph, g, _, c, _ = units[u]
            return (0 if ph == SHARED else g), c * COLS[ph]

        block = ctx.enter_context(nc.Block())

        @block.sync
        def _(sp):
            def load_x(b):
                sp.dma_start(xin, x[b * TB:(b + 1) * TB, :].rearrange("(t p) d -> p t d", p=P)).then_inc(x_loaded, 16)

            def load_w(w, source):
                if w >= 2:
                    sp.wait_ge(w_ready, w - 1)
                sp.dma_start(staged[:, w % 2, 0:source.shape[-1]], source).then_inc(w_loaded[w % 2], 16)

            load_x(0)
            for dst, src in ((convp[:], conv), (gate32[:], gate_w), (gbias[:], gate_b.partition_broadcast(P)),
                             *((ob[r:r + E + 1, :], out_bias) for r in BIAS_AT)):
                sp.dma_start(dst, src).then_inc(const_loaded, 16)
            x_after = {1: 1, 4: 2, 6: 3, 8: 4, 14: 5, 15: 6, 16: 7}

            def store_f(b):
                sp.wait_ge(final_ready, b + 1)
                sp.dma_start(f_rows[b * TB:(b + 1) * TB, :].rearrange("(t p) d -> p t d", p=P), nat
                             ).then_inc(stored, 16)

            for w in range(N_SPLITS):
                load_w(w, w_mix[w] if w < 8 else w_mlp[w - 8] if w < 16 else w_shared[w - 16])
                if w in x_after:
                    n = x_after[w]
                    if n <= NB:
                        sp.wait_ge(x_used, n)
                    else:
                        sp.wait_ge(x_added, n - NB)
                    load_x(n % NB)
            for b in range(NB):
                store_f(b)
            sp.wait_ge(slots_ready, 1)
            sp.dma_start(slot_dram, slot_i[:]).then_inc(slot_stored, 16)
            sp.wait_ge(slot_stored, 16)
            sp.dma_start(slot_row[:], slot_dram.rearrange("(a s) q -> a (s q)", a=1)).then_inc(slot_loaded, 16)
            sp.wait_ge(slot_loaded, 16)

            def load_slot(s, par):
                unit = sp.value_load(slot_row[0:1, bass.ds(s * 2 + 1, 1)], min_val=0, max_val=PER * (E - 1))
                for c in range(PER):
                    n = par * PER + c
                    sp.wait_ge(w_ready, s * PER + (N_SPLITS + c - 1))
                    stage = (N_SPLITS + n) % 2
                    sp.dma_start(staged[:, stage, 0:COLS[SHARED] + 2],
                                 w_moe[bass.ds(unit + c, 1), :, :].rearrange("a p n -> (a p) n")
                                 ).then_inc(w_loaded[stage], 16)

            def store_slot(s):
                sp.wait_ge(acc_added, s * NTS + (NT * N_RUNS + NTS))
                dst = y_rows.rearrange("(q p) d -> p q d", p=P)[:, bass.ds(s * NTS, NTS), :]
                sp.dma_start(dst, yout[:]).then_inc(stored, 16)

            late = 2
            for i in range(late):
                load_slot(i, i % 2)
            with sp.Fori(0, N_SLOTS - 1 - late, 2) as j:
                for i in range(2):
                    load_slot(j + (late + i), i)
                    store_slot(j + i)
            load_slot(N_SLOTS - 1, 0)
            store_slot(N_SLOTS - 1 - late)
            for i in range(SHARED_UNITS[1]):
                load_w(N_SPLITS + R_UNITS + i, w_shared[SHARED_UNITS[0] + i])
            for i in range(late):
                store_slot(N_SLOTS - late + i)
            for b in range(NB):
                for t in range(NT):
                    sp.wait_ge(acc_added, sums(N_RUNS + N_SLOTS + b) + t + 1)
                    sp.wait_ge(got_used, (TOP - 1) * NB * NT + b * NT + t + 1)
                    r = b * TB + t * P
                    sp.dma_start(out[r:r + P, :], acc[:, b, t, :]).then_inc(out_stored, 16)
            sp.wait_ge(out_stored, 16 * NB * NT)

        @block.gpsimd
        def _(pool):
            pool.memset(ident[:], 0.0).then_inc(pool_step, 1)
            pool.wait_ge(pool_step, 1)
            pool.affine_select(out=ident[:], in_=ident[:], compare_op=ALU.not_equal, fill=1.0, base=0,
                               pattern=[[-1, P]], channel_multiplier=1).then_inc(ident_ready, 1)
            pool.memset(ones16[:], 1.0).then_inc(pool_step, 1)
            pool.wait_ge(pool_step, 2)
            pool.affine_select(out=before16[:], in_=ones16[:], compare_op=ALU.is_gt, fill=0.0, base=0,
                               pattern=[[1, P]], channel_multiplier=-1).then_inc(pool_step, 1)
            pool.iota(token_no[:], pattern=[[P, NB * NT]], base=0, channel_multiplier=1).then_inc(pool_step, 1)
            pool.iota(first_place[:], pattern=[[T, E]], base=0, channel_multiplier=0,
                      allow_small_or_imprecise_dtypes=True).then_inc(pool_step, 1)
            pool.iota(expert_no[:], pattern=[[1, E]], base=0, channel_multiplier=0,
                      allow_small_or_imprecise_dtypes=True).then_inc(pool_step, 1)
            pool.iota(slot_no[:], pattern=[[0, 1]], base=0, channel_multiplier=1,
                      allow_small_or_imprecise_dtypes=True).then_inc(pool_step, 1)
            pool.memset(tokens[:], 0).then_inc(pool_step, 1)
            pool.wait_ge(pool_step, 8)
            pool.dma_start(token_at.rearrange("(p q) a -> p (q a)", p=P), tokens[:, 0:E * T // P]
                           ).then_inc(table_set, 16)
            pool.wait_ge(table_set, 16)
            for b in range(NB):
                pool.wait_ge(places_ready, b + 1)
                for t in range(NT):
                    for k in range(TOP):
                        pool.indirect_dma_start(
                            token_at, bass.IndirectOffsetOnAxis(ap=table_i[:, b, t, k:k + 1].bitcast(U32), axis=0),
                            token_no[:, b * NT + t:b * NT + t + 1], None).then_inc(table_set, 16)
            pool.wait_ge(table_set, 16 * (1 + NB * NT * TOP))
            pool.dma_start(tokens[:, 0:E * T // P], token_at.rearrange("(p q) a -> p (q a)", p=P)
                           ).then_inc(tokens_loaded, 16)
            pool.wait_ge(tokens_loaded, 16)
            pool.wait_ge(slot_loaded, 16)

            def gather(s, par):
                column = pool.value_load(slot_row[0:1, bass.ds(s * 2, 1)], min_val=0,
                                         max_val=(E - 1) * (T // P) + (MAX_SLOTS - 1) * NTS)
                pool.tensor_copy(tokens_now[:, par, :], tokens[:, bass.ds(column, NTS)]).then_inc(now_ready, 1)
                pool.wait_ge(stored, 16 * NB)
                pool.wait_ge(now_ready, s + 1)
                pool.sem_inc(gathering, 1)
                for t in range(NTS):
                    pool.indirect_dma_start(
                        rows[:, par, t, :], None, f_rows,
                        bass.IndirectOffsetOnAxis(ap=tokens_now[:, par, t:t + 1].bitcast(U32), axis=0)
                        ).then_inc(rows_loaded[par], 16)

            def rows_free(j, par):
                pool.wait_ge(filled, j * (2 * SLOT_ITEMS) + (2 * (N_ITEMS + SLOT_ITEMS * (par - 1) + 2) + 2))

            pool.wait_ge(freed, t_item(2, NB - 1, 1) + 1)
            gather(0, 0)
            gather(1, 1)
            late = 3
            with pool.Fori(0, N_SLOTS - 2 - late, 2) as j:
                for par in range(2):
                    rows_free(j, par)
                    gather(j + (2 + par), par)
            for i in range(N_SLOTS - late, N_SLOTS - 1):
                rows_free(i - 2 - i % 2, i % 2)
                gather(i, i % 2)
            for n in range(NB * NT * TOP):
                k, b, t = got_tile(n)
                if n == ROWBUFS:
                    rows_free(N_SLOTS - 3, 0)
                    gather(N_SLOTS - 1, 0)
                if n % (NB * NT) == 0:
                    pool.wait_ge(stored, 16 * (NB + FIRST_SLOTS[k]))
                if n >= ROWBUFS:
                    pool.wait_ge(got_used, n - ROWBUFS + 1)
                pool.indirect_dma_start(
                    got(n), None, y_rows[0:FIRST_SLOTS[k] * SLOT, :],
                    bass.IndirectOffsetOnAxis(ap=out_i[:, b, t, k:k + 1].bitcast(U32), axis=0)
                    ).then_inc(got_loaded[n % ROWBUFS], 16)

        @block.tensor
        def _(pe):
            def up(slot, buf, base, rows_t, n_tok=TB):
                for m in range(2):
                    for k in range(KD):
                        w0 = base + (m * KD + k) * P
                        for n, (pw, px) in enumerate(PASSES):
                            mm = pe.matmul(ring[:, 2 * slot + m, 0:n_tok], weights[:, buf, pw, w0:w0 + P],
                                           rows_t(px, k), start=(k == 0 and n == 0), stop=(k == KD - 1 and n == 2))
                    mm.then_inc(filled, 1)

            def down(hslot, chunks, buf, base, first, last, read, n_tiles=NT, bias_of=None):
                for t in range(n_tiles):
                    if first and read is not None:
                        pe.wait_ge(acc_added, read[t])
                    for c in range(chunks):
                        w0 = base + UP + c * D
                        for n, (ph, pw) in enumerate(PASSES):
                            mm = pe.matmul(downs[:, t, :], hidden[:, hslot, ph, c, t * P:(t + 1) * P],
                                           weights[:, buf, pw, w0:w0 + D], start=(first and c == 0 and n == 0),
                                           stop=(last and bias_of is None and c == chunks - 1 and n == 2))
                    if bias_of is not None:
                        mm = pe.matmul(downs[:, t, :], cwt(bias_of)[:, t * P:(t + 1) * P], ob16[:],
                                       start=False, stop=True)
                    mm.then_inc(tile_done, 1)

            def slot_for(item):
                if item >= 2:
                    pe.wait_ge(freed, item - 1)
                return item % 2

            def transpose_rows(slot, source, h, n_tiles=NT):
                for k in range(2):
                    for t in range(n_tiles):
                        d0 = (2 * h + k) * P
                        tr = pe.transpose(ring[:, 2 * slot + k, t * P:(t + 1) * P], source[:, t, d0:d0 + P], ident[:])
                    tr.then_inc(filled, 1)

            def up_unit(step):
                u = step[1]
                ph, g, b, c, _ = units[u]
                s = slot_for(item_of[step])
                if g == 0 and c == 0:
                    pe.wait_ge(freed, t_item(ph, b, 1) + 1)
                if b == 0:
                    if ph != SHARED:
                        pe.wait_ge(w_ready, 8 * ph + 4 * g + c + 1)
                    elif g == 0:
                        pe.wait_ge(w_ready, 16 + c + 1)
                    else:
                        pe.wait_ge(w_ready, N_SPLITS + R_UNITS + c + 1)
                up(s, *unit_weights(u), lambda px, k: xt[:, b, px, k, :])

            def sums_read(run):
                return [min(sums(run - 1) + t + 1, sums(run)) for t in range(NT)]

            def down_unit(u):
                ph, g, b, c, last = units[u]
                if ph == MLP:
                    pe.wait_ge(freed, item_of[("U", u)] + 1)
                else:
                    pe.wait_ge(h_ready, gated(u) + 1)
                biased = last and (ph, g) == (SHARED, 0)
                if biased:
                    pe.wait_ge(freed, item_of[("P", b)] + 1)
                down(seq(u) % HSLOTS, 1 + (ph == MLP), *unit_weights(u), c == 0, last,
                     sums_read(run_of[u]) if run_of[u] else None, bias_of=b if biased else None)

            def transpose_slot(t, l, h):
                item = t * (2 * SLOT_ITEMS) + (N_ITEMS + SLOT_ITEMS * l + h)
                pe.wait_ge(freed, item - 1)
                par = (l + 1) % 2
                pe.wait_ge(rows_loaded[par], t * (16 * NTS) + 16 * NTS * ((l + 1) // 2 + 1))
                transpose_rows((N_ITEMS + SLOT_ITEMS * l + h) % 2, rows[:, par], h, NTS)

            def up_slot(t, item, n):
                pe.wait_ge(freed, t * (2 * SLOT_ITEMS) + (item - 1))
                pe.wait_ge(w_ready, t * (2 * PER) + (N_SPLITS + n + 1))
                buf = (n // PER + 1) % 2
                up(item % 2, buf, n % PER * COLS[SHARED],
                   lambda px, k: weights[:, buf, px, XG + k * SLOT:XG + (k + 1) * SLOT], SLOT)

            def down_slot(t, n):
                pe.wait_ge(h_ready, t * (2 * PER) + (R0 + n + 1))
                c = n % PER
                down((N_AHEAD + n) % HSLOTS, 1, (n // PER + 1) % 2, c * COLS[SHARED], c == 0, c == PER - 1,
                     [t * (2 * NTS) + (NT * N_RUNS + NTS * (n // PER - 1) + k + 1) for k in range(NTS)], NTS)

            def walk(order):
                for step in order:
                    kind = step[0]
                    if kind == "T":
                        _, n, b, h = step
                        s = slot_for(item_of[step])
                        if n < 2:
                            pe.wait_ge(nat_ready, NB * n + b + 1)
                        else:
                            pe.wait_ge(final_ready, b + 1)
                        transpose_rows(s, nat, h)
                    elif kind == "U":
                        up_unit(step)
                    elif kind == "D":
                        down_unit(step[1])
                    elif kind == "G":
                        b = step[1]
                        s = slot_for(item_of[step])
                        pe.wait_ge(freed, t_item(2, b, 1) + 1)
                        pe.wait_ge(gate_ready, 1)
                        for t in range(NT):
                            for k in range(KD):
                                for n, (px, pw) in enumerate(PASSES):
                                    mm = pe.matmul(ring[:, 2 * s + t // 2, t % 2 * E:(t % 2 + 1) * E],
                                                   xt[:, b, px, k, t * P:(t + 1) * P], gate16[:, pw, k, :],
                                                   start=(k == 0 and n == 0), stop=(k == KD - 1 and n == 2))
                            if t % 2:
                                mm.then_inc(filled, 1)
                    elif kind == "P":
                        s = slot_for(item_of[step])
                        pe.wait_ge(mask_ready, step[1] + 1)
                        pe.matmul(ring[:, 2 * s, 0:NT * E], before16[:], mask16[:].rearrange("p t e -> p (t e)"),
                                  start=True, stop=False)
                        pe.matmul(ring[:, 2 * s, 0:NT * E], ones16[:],
                                  prior16[:, 0:NT, :].rearrange("p t e -> p (t e)"),
                                  start=False, stop=True)
                        pe.matmul(ring[:, 2 * s, NT * E:(NT + 1) * E], ones16[:], prior16[:, NT, :],
                                  start=True, stop=True).then_inc(filled, 1)
                        pe.wait_ge(cw_ready, step[1] + 1)
                        for t in range(NT):
                            tr = pe.transpose(ring[0:BIAS_ROWS, 2 * s + 1, :].bitcast(F16)[:, t * P:(t + 1) * P],
                                              cw16[:, t, :], ident16[:])
                        tr.then_inc(filled, 1)
                    elif kind == "RT":
                        s = slot_for(item_of[step])
                        pe.wait_ge(rows_loaded[0], 16 * NTS)
                        transpose_rows(s, rows[:, 0], step[2], NTS)
                    elif kind == "RU":
                        if step[1] == 0:
                            pe.wait_ge(freed, item_of[("RT", 0, 1)] + 1)
                        up_slot(0 if step[1] < 2 else N_LOOP // 2,
                                item_of[step] if step[1] < 2 else N_ITEMS, step[1] % (2 * PER))
                    elif kind == "RD":
                        down_slot(N_LOOP // 2, step[1] % (2 * PER))

            pe.wait_ge(ident_ready, 1)
            pe.wait_ge(pool_step, 8)
            walk(steps)
            with pe.Fori(0, N_LOOP // 2) as t:
                for l in range(2):
                    i, n = N_ITEMS + SLOT_ITEMS * l, PER * l
                    transpose_slot(t, l, 0)
                    down_slot(t, n)
                    transpose_slot(t, l, 1)
                    up_slot(t, i + 2, n + 2)
                    down_slot(t, n + 1)
                    up_slot(t, i + 3, n + 3)
                    down_slot(t, n + 2)
                    up_slot(t, i + 4, n + 4)
            walk(tail)

        @block.scalar
        def _(act):
            roots = 0
            exps = 0
            centers = 0

            def root():
                nonlocal roots
                roots += 1
                act.wait_ge(sqrt_in, roots)
                act.activation(small[:, 1, :], small[:, 0, :], ACT.Sqrt).then_inc(sqrt_done, 1)

            def centered(src, dst):
                nonlocal centers
                centers += 1
                act.wait_ge(center_ready, centers)
                for t in range(NT):
                    ins = act.activation(dst[:, t, :], src[:, t, :], ACT.Identity, scale=small[:, 2, t:t + 1],
                                         bias=small[:, 3, t:t + 1])
                return ins

            def split_high(stage, loads, free_at, buf, base, cols):
                act.wait_ge(w_loaded[stage], loads)
                if free_at is not None:
                    act.wait_ge(tile_done, free_at)
                act.activation(weights[:, buf, 0, base:base + cols], staged[:, stage, 0:cols], ACT.Copy,
                               scale=WS).then_inc(w_high, 1)

            def gated_unit(fill, slot, silu_slot, bias, read, hslot, done, n_tok=TB):
                act.wait_ge(filled, fill)
                act.activation(sil[:, silu_slot, 0:n_tok], ring[:, 2 * slot, 0:n_tok], ACT.Silu, scale=1 / WS,
                               bias=bias).then_inc(silu_ready, 1)
                act.wait_ge(freed, read)
                act.wait_ge(tile_done, done)
                act.activation(hidden[:, hslot, 0, 0, 0:n_tok], tmp[:, silu_slot, 0:n_tok], ACT.Copy,
                               scale=1 / WS).then_inc(h_high, 1)

            def transposed_slot(t, l, h):
                c0 = N_ITEMS + SLOT_ITEMS * l + h
                act.wait_ge(filled, t * (4 * SLOT_ITEMS) + (2 * c0 + 2))
                x0 = XG + 2 * h * SLOT
                act.activation(weights[:, l % 2, 0, x0:x0 + 2 * SLOT].rearrange("p (k t) -> p k t", k=2),
                               ring[:, 2 * (c0 % 2):2 * (c0 % 2) + 2, 0:SLOT], ACT.Copy).then_inc(t_high, 1)

            def unit_slot(t, item, n):
                gated_unit(t * (4 * SLOT_ITEMS) + (2 * item + 1), item % 2, (R0 + n) % 2,
                           ebias[:, (n // PER + 1) % 2, n % PER, 0:1],
                           t * (2 * SLOT_ITEMS) + (item + 1), (N_AHEAD + n) % HSLOTS,
                           t * (2 * PER * NTS) + tiles(N_AHEAD + n - HSLOTS + 1), SLOT)

            def split_slot(t, n):
                w = N_SPLITS + n
                split_high(w % 2, t * (PER * 16) + 16 * (w // 2 + 1),
                           t * (2 * PER * NTS) + tiles(N_AHEAD + n - 2 * PER + 1), (n // PER + 1) % 2,
                           n % PER * COLS[SHARED], COLS[SHARED])

            def copy_slot(t, l):
                act.wait_ge(stored, t * 32 + 16 * (NB + l))
                for k in range(NTS):
                    act.wait_ge(tile_done, t * (2 * PER * NTS) + (tiles(N_AHEAD + PER * l + 2) + k + 1))
                    act.activation(yout[:, k, :], downs[:, k, :], ACT.Copy, scale=1 / WS).then_inc(acc_added, 1)

            def walk(order):
                nonlocal exps
                for step in order:
                    kind = step[0]
                    if kind == "split":
                        w = step[1]
                        buf, j, cols = split_place(w)
                        split_high(w % 2, 16 * (w // 2 + 1), split_after(w) or None, buf, j * cols, cols)
                    elif kind in ("stats", "squares"):
                        root()
                    elif kind == "center":
                        centered(xin, acc[:, step[1]]).then_inc(x_used, 1)
                    elif kind == "final":
                        b = step[1]
                        if b:
                            act.wait_ge(filled, 2 * t_item(2, b - 1, 1) + 2)
                            act.wait_ge(stored, 16 * b)
                        centered(acc[:, b], nat).then_inc(final_ready, 1)
                    elif kind == "T":
                        _, n, b, h = step
                        s = item_of[step] % 2
                        act.wait_ge(filled, 2 * item_of[step] + 2)
                        act.activation(xt[:, b, 0, 2 * h:2 * h + 2, :], ring[:, 2 * s:2 * s + 2, :],
                                       ACT.Copy).then_inc(t_high, 1)
                    elif kind == "U":
                        u = step[1]
                        ph, g, b, c, _ = units[u]
                        item = item_of[step]
                        s = item % 2
                        if ph == MIX:
                            act.wait_ge(filled, 2 * item + 1)
                            if u >= 2:
                                act.wait_ge(freed, item_of[("U", u - 2)] + 1)
                            act.activation(xpad[:, u % 2, TAPS - 1:TAPS - 1 + TB], ring[:, 2 * s, :], ACT.Copy,
                                           scale=1 / WS)
                            cc = 4 * g + c
                            act.activation(tmp[:, u % 2, :], ring[:, 2 * s, :], ACT.Identity,
                                           scale=convp[:, cc, TAPS - 1:TAPS], bias=convp[:, cc, TAPS:TAPS + 1]
                                           ).then_inc(xp_ready, 1)
                            act.wait_ge(filled, 2 * item + 2)
                            act.activation(sil[:, u % 2, :], ring[:, 2 * s + 1, :], ACT.Silu,
                                           scale=1 / WS)
                            act.wait_ge(conv_ready, u + 1)
                            act.activation(tmp[:, u % 2, :], tmp[:, u % 2, :], ACT.Silu).then_inc(conv_silu, 1)
                            act.wait_ge(freed, item + 1)
                            if u >= HSLOTS:
                                act.wait_ge(tile_done, tiles(u - HSLOTS + 1))
                            act.activation(hidden[:, u % HSLOTS, 0, 0, :], h32[:], ACT.Copy).then_inc(h_high, 1)
                        elif ph == MLP:
                            act.wait_ge(filled, 2 * item + 2)
                            act.wait_ge(tile_done, tiles(u - HSLOTS + 1))
                            act.activation(hidden[:, u % HSLOTS, 0, :, :], ring[:, 2 * s:2 * s + 2, :],
                                           ACT.Relu).then_inc(h_high, 1)
                        else:
                            gated_unit(2 * item + 1, s, gated(u) % 2, ebias[:, 0, c, 0:1], item + 1,
                                       seq(u) % HSLOTS, tiles(seq(u) - HSLOTS + 1))
                    elif kind == "evac" and units[step[1]][:2] == (MLP, 1):
                        root()
                    elif kind == "G":
                        exps += 1
                        act.wait_ge(exp_in, exps)
                        act.activation(prob[:], score[:], ACT.Exp).then_inc(exp_done, 1)
                    elif kind == "RT":
                        transposed_first(item_of[step], step[2])
                    elif kind == "RU":
                        if step[1] < 2:
                            unit_slot(0, item_of[step], step[1])
                        else:
                            unit_slot(N_LOOP // 2, N_ITEMS, step[1] % (2 * PER))
                    elif kind == "Revac":
                        copy_slot(N_LOOP // 2, 0)

            def transposed_first(item, h):
                act.wait_ge(filled, 2 * item + 2)
                x0 = XG + 2 * h * SLOT
                act.activation(weights[:, 1, 0, x0:x0 + 2 * SLOT].rearrange("p (k t) -> p k t", k=2),
                               ring[:, 2 * (item % 2):2 * (item % 2) + 2, 0:SLOT], ACT.Copy).then_inc(t_high, 1)

            walk(steps[:LEAD])
            act.wait_ge(const_loaded, 16 * 6)
            act.activation(gate16[:, 0], gate32[:], ACT.Copy, scale=WS).then_inc(gate_high, 1)
            act.wait_ge(const_scaled, 1)
            walk(steps[LEAD:])
            with act.Fori(0, N_LOOP // 2) as t:
                for l in range(2):
                    i, n = N_ITEMS + SLOT_ITEMS * l, PER * l
                    transposed_slot(t, l, 0)
                    transposed_slot(t, l, 1)
                    split_slot(t, n + 6)
                    unit_slot(t, i + 2, n + 2)
                    split_slot(t, n + 7)
                    unit_slot(t, i + 3, n + 3)
                    copy_slot(t, l)
                    split_slot(t, n + 8)
                    unit_slot(t, i + 4, n + 4)
            walk(tail)

        @block.vector
        def _(dve):
            steps_done = 0
            roots = 0

            def link(ins):
                nonlocal steps_done
                steps_done += 1
                ins.then_inc(dve_step, 1)
                dve.wait_ge(dve_step, steps_done)

            def root():
                nonlocal roots
                roots += 1
                dve.wait_ge(sqrt_done, roots)

            def split_low(stage, buf, base, cols, high, bias):
                dve.wait_ge(w_high, high)
                if bias is not None:
                    dve.tensor_copy(bias[:, 0:1], staged[:, stage, cols:cols + 1])
                    dve.tensor_scalar(bias[:, 1:2], staged[:, stage, cols + 1:cols + 2], WS, None, ALU.mult)
                dve.scalar_tensor_tensor(out=weights[:, buf, 1, base:base + cols], in0=staged[:, stage, 0:cols],
                                         scalar=WS, in1=weights[:, buf, 0, base:base + cols], op0=ALU.mult,
                                         op1=ALU.subtract).then_inc(w_ready, 1)

            def statistics(src):
                for t in range(NT):
                    ins = dve.bn_stats(stats[:, t, :], src[:, t, :])
                link(ins)
                for t in range(NT):
                    ins = dve.bn_aggr(mv[:, t, :], stats[:, t, :])
                link(ins)
                dve.tensor_scalar(small[:, 0, :], mv[:, :, 1], EPS, None, ALU.add).then_inc(sqrt_in, 1)

            def center():
                root()
                link(dve.reciprocal(small[:, 2, :], small[:, 1, :]))
                dve.scalar_tensor_tensor(out=small[:, 3, :], in0=mv[:, :, 0], scalar=-1.0, in1=small[:, 2, :],
                                         op0=ALU.mult, op1=ALU.mult).then_inc(center_ready, 1)

            def squares(n, b):
                if n or b:
                    before = (n, b - 1) if b else (n - 1, NB - 1)
                    dve.wait_ge(filled, 2 * t_item(*before, 1) + 2)
                for t in range(NT):
                    ins = dve.tensor_tensor_reduce(nat[:, t, :], acc[:, b, t, :], acc[:, b, t, :], 1.0, 0.0, ALU.mult,
                                                   ALU.add, small[:, 0, t:t + 1])
                ins.then_inc(sqrt_in, 1)

            def scale_rows(src):
                root()
                link(dve.tensor_scalar(small[:, 4, :], small[:, 1, :], 1e-12, None, ALU.max))
                link(dve.reciprocal(small[:, 5, :], small[:, 4, :]))
                for t in range(NT):
                    ins = dve.tensor_scalar(nat[:, t, :], src[:, t, :], small[:, 5, t:t + 1], float(D) ** 0.5,
                                            ALU.mult, ALU.mult)
                ins.then_inc(nat_ready, 1)

            def mixer_unit(u, item):
                cc = 4 * units[u][1] + units[u][3]
                dve.wait_ge(xp_ready, u + 1)
                for tap in range(TAPS - 1):
                    ins = dve.scalar_tensor_tensor(out=tmp[:, u % 2, :], in0=xpad[:, u % 2, tap:tap + TB],
                                                   scalar=convp[:, cc, tap:tap + 1], in1=tmp[:, u % 2, :],
                                                   op0=ALU.mult, op1=ALU.add)
                    if tap < TAPS - 2:
                        link(ins)
                ins.then_inc(conv_ready, 1)
                dve.wait_ge(conv_silu, u + 1)
                dve.tensor_tensor(h32[:], tmp[:, u % 2, :], sil[:, u % 2, :], ALU.mult).then_inc(freed, 1)
                dve.wait_ge(h_high, u + 1)
                dve.tensor_tensor(hidden[:, u % HSLOTS, 1, 0, :], h32[:], hidden[:, u % HSLOTS, 0, 0, :],
                                  ALU.subtract).then_inc(h_ready, 1)

            def gated_unit(fill, slot, silu_at, silu_slot, bias, hslot, high, n_tok=TB):
                dve.wait_ge(filled, fill)
                dve.wait_ge(silu_ready, silu_at)
                dve.scalar_tensor_tensor(out=tmp[:, silu_slot, 0:n_tok], in0=ring[:, 2 * slot + 1, 0:n_tok],
                                         scalar=bias, in1=sil[:, silu_slot, 0:n_tok], op0=ALU.add, op1=ALU.mult
                                         ).then_inc(freed, 1)
                dve.wait_ge(h_high, high)
                dve.scalar_tensor_tensor(out=hidden[:, hslot, 1, 0, 0:n_tok], in0=tmp[:, silu_slot, 0:n_tok],
                                         scalar=1 / WS, in1=hidden[:, hslot, 0, 0, 0:n_tok], op0=ALU.mult,
                                         op1=ALU.subtract).then_inc(h_ready, 1)

            def gate(b, item):
                s = item % 2
                dve.wait_ge(filled, 2 * item + 2)
                dve.tensor_scalar(score[:].rearrange("p (a t) e -> p a (t e)", a=2),
                                  ring[:, 2 * s:2 * s + 2, 0:2 * E], 1 / WS, None, ALU.mult).then_inc(freed, 1)
                dve.wait_ge(freed, item + 1)
                link(dve.tensor_reduce(small[:, 0, :], score[:], AX.X, ALU.max))
                dve.tensor_tensor(score[:], score[:], small[:, 0, :].unsqueeze(2).to_broadcast([P, NT, E]),
                                  ALU.subtract).then_inc(exp_in, 1)
                dve.wait_ge(exp_done, b + 1)
                link(dve.tensor_reduce(small[:, 2, :], prob[:], AX.X, ALU.add))
                link(dve.reciprocal(small[:, 3, :], small[:, 2, :]))
                link(dve.tensor_tensor(prob[:], prob[:], small[:, 3, :].unsqueeze(2).to_broadcast([P, NT, E]),
                                       ALU.mult))
                link(dve.tensor_tensor(biased[:, :, 0:E], prob[:], gbias[:].unsqueeze(1).to_broadcast([P, NT, E]),
                                       ALU.add))
                for t in range(NT):
                    ins = dve.max(best[:, t, :], biased[:, t, :])
                link(ins)
                link(dve.memset(best[:, :, TOP:8], FLOOR))
                for t in range(NT):
                    ins = dve.match_replace(marked[:, t, :], best[:, t, :], biased[:, t, :], TAKEN)
                link(ins)
                link(dve.tensor_tensor(mask[:], marked[:, :, 0:E], biased[:, :, 0:E], ALU.not_equal))
                link(dve.tensor_tensor(cw[:], mask[:], prob[:], ALU.mult))
                high, high_too, low = (cw16[:, :, r:r + E] for r in BIAS_AT)
                dve.tensor_scalar(high_too, cw[:], WS, None, ALU.mult)
                link(dve.tensor_scalar(high, cw[:], WS, None, ALU.mult))
                dve.scalar_tensor_tensor(out=low, in0=cw[:], scalar=WS, in1=high, op0=ALU.mult, op1=ALU.subtract
                                         ).then_inc(cw_ready, 1)
                if b:
                    dve.wait_ge(filled, 2 * item_of[("P", b - 1)] + 2)
                    link(dve.tensor_copy(prior16[:, 0, :], prior16[:, NT, :]))
                dve.tensor_copy(mask16[:], mask[:])
                for t in range(NT):
                    ins = dve.tensor_tensor(prior16[:, t + 1, :], prior16[:, t, :], mask[:, t, :], ALU.add)
                    if t + 1 < NT:
                        link(ins)
                ins.then_inc(mask_ready, 1)

            def running_sum(src, bufs):
                step = 1
                for n in range(4):
                    dst = bufs[n % 2]
                    dve.tensor_copy(dst[..., 0:step], src[..., 0:step])
                    link(dve.tensor_tensor(dst[..., step:E], src[..., step:E], src[..., 0:E - step], ALU.add))
                    src, step = dst, 2 * step
                return src

            def ranks(b, item):
                s = item % 2
                dve.wait_ge(filled, 2 * item + 2)
                if b == NB - 1:
                    dve.tensor_copy(count[:], ring[:, 2 * s, NT * E:(NT + 1) * E])
                dve.tensor_copy(cwt(b), ring[0:BIAS_ROWS, 2 * s + 1, :].bitcast(F16)[:, 0:TB])
                dve.tensor_tensor(place[:], ring[:, 2 * s, 0:NT * E].rearrange("p (t e) -> p t e", t=NT),
                                  first_place[:].unsqueeze(1).to_broadcast([P, NT, E]), ALU.add).then_inc(freed, 1)
                dve.wait_ge(freed, item + 1)

            def places(b):
                upto_here = running_sum(mask[:], (rank[:, 0], rank[:, 1]))
                dve.wait_ge(cw_ready, b + 1)
                link(dve.tensor_tensor(rank[:, 0], upto_here, mask[:], ALU.mult))

                def picked(src, dst):
                    for k in range(TOP):
                        link(dve.scalar_tensor_tensor(out=pick[:, k % 2], in0=rank[:, 0], scalar=float(k + 1),
                                                      in1=src[:], op0=ALU.is_equal, op1=ALU.mult))
                        ins = dve.tensor_reduce(dst[:, b, :, k], pick[:, k % 2], AX.X, ALU.add)
                    link(ins)

                picked(place, place_k)
                link(dve.tensor_copy(place_i[:], place_k[:, b]))
                dve.tensor_scalar(low_i[:], place_i[:], P - 1, None, ALU.bitwise_and)
                link(dve.tensor_scalar(high_i[:], place_i[:], 7, None, ALU.logical_shift_right))
                dve.scalar_tensor_tensor(out=table_i[:, b], in0=low_i[:], scalar=float(E * T // P), in1=high_i[:],
                                         op0=ALU.mult, op1=ALU.add).then_inc(places_ready, 1)
                picked(cw, weight_k)

            def slot_table():
                link(dve.tensor_scalar(slots_of[:], count[:], 0.0, None, ALU.is_gt))
                for j in range(1, MAX_SLOTS):
                    link(dve.scalar_tensor_tensor(out=slots_of[:], in0=count[:], scalar=float(SLOT * j),
                                                  in1=slots_of[:], op0=ALU.is_gt, op1=ALU.add))
                total = running_sum(slots_of[:], (upto[:, 0], upto[:, 1]))
                link(dve.tensor_scalar(pick[:, 0, 0, :], total, slot_no[:, 0:1], None, ALU.is_le))
                link(dve.tensor_reduce(slot_f[:, 0:1], pick[:, 0, 0, :], AX.X, ALU.add))
                link(dve.tensor_scalar(slot_f[:, 0:1], slot_f[:, 0:1], float(E - 1), None, ALU.min))
                link(dve.tensor_tensor(pick[:, 0, 1, :], total, slots_of[:], ALU.subtract))
                dve.scalar_tensor_tensor(out=shift[:], in0=pick[:, 0, 1, :], scalar=float(SLOT), in1=first_place[:],
                                         op0=ALU.mult, op1=ALU.subtract)
                link(dve.scalar_tensor_tensor(out=pick[:, 0, 2, :], in0=expert_no[:], scalar=slot_f[:, 0:1],
                                              in1=pick[:, 0, 1, :], op0=ALU.is_equal, op1=ALU.mult))
                link(dve.tensor_reduce(slot_f[:, 1:2], pick[:, 0, 2, :], AX.X, ALU.add))
                link(dve.tensor_tensor(slot_f[:, 2:3], slot_no[:], slot_f[:, 1:2], ALU.subtract))
                link(dve.tensor_scalar(slot_f[:, 2:3], slot_f[:, 2:3], float(MAX_SLOTS - 1), float(NTS), ALU.min,
                                       ALU.mult))
                link(dve.scalar_tensor_tensor(out=slot_f[:, 3:4], in0=slot_f[:, 0:1], scalar=float(T // P),
                                              in1=slot_f[:, 2:3], op0=ALU.mult, op1=ALU.add))
                dve.tensor_copy(slot_i[:, 0:1], slot_f[:, 3:4])
                dve.tensor_scalar(slot_i[:, 1:2], slot_f[:, 0:1], float(PER), None, ALU.mult).then_inc(slots_ready, 1)

            def out_rows(b):
                eq = h32[:, 0:NT * TOP * E].rearrange("p (n e) -> p n e", e=E)
                link(dve.tensor_copy(place_i[:], place_k[:, b]))
                link(dve.tensor_scalar(low_i[:], place_i[:], T.bit_length() - 1, None, ALU.logical_shift_right))
                link(dve.tensor_copy(expert_f[:], low_i[:].rearrange("p t k -> p (t k)")))
                link(dve.tensor_tensor(eq, expert_f[:].unsqueeze(2).to_broadcast([P, NT * TOP, E]),
                                       expert_no[:].unsqueeze(1).to_broadcast([P, NT * TOP, E]), ALU.is_equal))
                link(dve.tensor_tensor(eq, eq, shift[:].unsqueeze(1).to_broadcast([P, NT * TOP, E]), ALU.mult))
                link(dve.tensor_reduce(expert_f[:], eq, AX.X, ALU.add))
                link(dve.tensor_tensor(out_i[:, b].rearrange("p t k -> p (t k)"), expert_f[:],
                                       place_k[:, b].rearrange("p t k -> p (t k)"), ALU.add))

            def transposed_low(s, high, buf, h):
                dve.wait_ge(t_high, high)
                x0 = XG + 2 * h * SLOT
                parts = [weights[:, buf, p, x0:x0 + 2 * SLOT].rearrange("p (k t) -> p k t", k=2) for p in range(2)]
                dve.tensor_tensor(parts[1], ring[:, 2 * s:2 * s + 2, 0:SLOT], parts[0], ALU.subtract).then_inc(freed, 1)

            def unit_slot(t, item, n):
                gated_unit(t * (4 * SLOT_ITEMS) + (2 * item + 2), item % 2,
                           t * (2 * PER) + (R0 - N_MIX + n + 1), (R0 + n) % 2,
                           ebias[:, (n // PER + 1) % 2, n % PER, 1:2], (N_AHEAD + n) % HSLOTS,
                           t * (2 * PER) + (N_AHEAD + n + 1), SLOT)

            def split_slot(t, n):
                w = N_SPLITS + n
                buf = (n // PER + 1) % 2
                split_low(w % 2, buf, n % PER * COLS[SHARED], COLS[SHARED], t * (2 * PER) + (w + 1),
                          ebias[:, buf, n % PER])

            adds = 0

            def add_output(n):
                nonlocal adds
                k, b, t = got_tile(n)
                dve.wait_ge(got_loaded[n % ROWBUFS], 16 * (n // ROWBUFS + 1))
                if k:
                    dve.wait_ge(got_used, n - NB * NT + 1)
                dve.scalar_tensor_tensor(out=acc[:, b, t, :], in0=got(n), scalar=weight_k[:, b, t, k:k + 1],
                                         in1=acc[:, b, t, :], op0=ALU.mult, op1=ALU.add).then_inc(got_used, 1)
                adds = n + 1

            def walk(order):
                for step in order:
                    kind = step[0]
                    if kind == "split":
                        w = step[1]
                        buf, j, cols = split_place(w)
                        split_low(w % 2, buf, j * cols, cols, w + 1, ebias[:, buf, j] if w >= 16 else None)
                    elif kind == "stats":
                        dve.wait_ge(x_loaded, 16 * (step[1] + 1))
                        statistics(xin)
                    elif kind in ("center", "final"):
                        center()
                    elif kind == "squares":
                        _, n, b = step
                        if n == 0:
                            dve.wait_ge(x_used, b + 1)
                        squares(n, b)
                    elif kind == "scale":
                        scale_rows(acc[:, step[2]])
                    elif kind == "X":
                        b = step[1]
                        dve.wait_ge(x_loaded, 16 * (NB + b + 1))
                        dve.tensor_tensor(acc[:, b], acc[:, b], xin, ALU.add).then_inc(x_added, 1)
                        dve.wait_ge(x_added, b + 1)
                    elif kind == "T":
                        _, n, b, h = step
                        s = item_of[step] % 2
                        dve.wait_ge(t_high, 2 * (NB * n + b) + h + 1)
                        dve.tensor_tensor(xt[:, b, 1, 2 * h:2 * h + 2, :], ring[:, 2 * s:2 * s + 2, :],
                                          xt[:, b, 0, 2 * h:2 * h + 2, :], ALU.subtract).then_inc(freed, 1)
                    elif kind == "U":
                        u = step[1]
                        ph, g, b, c, _ = units[u]
                        item = item_of[step]
                        s = item % 2
                        if ph == MIX:
                            mixer_unit(u, item)
                        elif ph == MLP:
                            dve.wait_ge(h_high, u + 1)
                            dve.scalar_tensor_tensor(out=hidden[:, u % HSLOTS, 1, :, :],
                                                     in0=ring[:, 2 * s:2 * s + 2, :], scalar=0.0,
                                                     in1=hidden[:, u % HSLOTS, 0, :, :], op0=ALU.max,
                                                     op1=ALU.subtract).then_inc(freed, 1)
                        else:
                            gated_unit(2 * item + 2, s, gated(u) - N_MIX + 1, gated(u) % 2, ebias[:, 0, c, 1:2],
                                       seq(u) % HSLOTS, seq(u) + 1)
                    elif kind == "evac":
                        u = step[1]
                        ph, g, b, c, _ = units[u]
                        scale = 1 / WS ** 2 if ph == MLP else 1 / WS
                        if adds:
                            dve.wait_ge(got_used, adds)
                        for t in range(NT):
                            dve.wait_ge(tile_done, tiles(seq(u)) + t + 1)
                            dve.scalar_tensor_tensor(out=acc[:, b, t, :], in0=downs[:, t, :], scalar=scale,
                                                     in1=acc[:, b, t, :], op0=ALU.mult, op1=ALU.add
                                                     ).then_inc(acc_added, 1)
                        dve.wait_ge(acc_added, sums(run_of[u] + 1))
                        if (ph, g) == (MLP, 1):
                            statistics(acc[:, b])
                    elif kind == "G":
                        gate(step[1], item_of[step])
                    elif kind == "P":
                        ranks(step[1], item_of[step])
                    elif kind == "places":
                        places(step[1])
                    elif kind == "slots":
                        slot_table()
                    elif kind == "rows":
                        out_rows(step[1])
                    elif kind == "RT":
                        item = item_of[step]
                        transposed_low(item % 2, 24 + step[2] + 1, 1, step[2])
                    elif kind == "RU":
                        if step[1] < 2:
                            unit_slot(0, item_of[step], step[1])
                        else:
                            unit_slot(N_LOOP // 2, N_ITEMS, step[1] % (2 * PER))
                    elif kind == "C":
                        add_output(step[1])

            dve.memset(xpad[:], 0.0)
            dve.memset(biased[:], FLOOR)
            link(dve.memset(cw16[:], 0.0))
            for r in BIAS_AT[0:2]:
                dve.memset(cw16[:, :, r + E:r + E + 1], WS)
            link(dve.memset(ob16[:], 0.0))
            dve.wait_ge(ident_ready, 1)
            dve.tensor_copy(ident16[:], ident[:])
            dve.memset(prior16[:], 0.0)
            walk(steps[:LEAD])
            dve.wait_ge(const_loaded, 16 * 6)
            dve.tensor_scalar(convp[:, :, TAPS - 1:TAPS], convp[:, :, TAPS - 1:TAPS], 1 / WS, None, ALU.mult
                              ).then_inc(const_scaled, 1)
            high, low, high_too = (slice(r, r + E + 1) for r in BIAS_AT)
            for part in (high, low, high_too):
                ins = dve.tensor_copy(ob16[part, :], ob[part, :])
            link(ins)
            dve.tensor_tensor(ob16[low, :], ob[low, :], ob16[low, :], ALU.subtract)
            dve.wait_ge(pool_step, 8)
            dve.wait_ge(gate_high, 1)
            dve.scalar_tensor_tensor(out=gate16[:, 1], in0=gate32[:], scalar=WS, in1=gate16[:, 0], op0=ALU.mult,
                                     op1=ALU.subtract).then_inc(gate_ready, 1)
            walk(steps[LEAD:])

            def slot(t, l, early):
                i, n = N_ITEMS + SLOT_ITEMS * l, PER * l
                for h in range(2):
                    transposed_low((i + h) % 2, t * 4 + (24 + 2 * (l + 1) + h + 1), l % 2, h)
                for c in range(2, 2 + PER):
                    split_slot(t, n + c + 4)
                    unit_slot(t, i + c, n + c)
                    for _ in range(early):
                        add_output(adds)

            with dve.Fori(0, EARLY_FROM // 2) as t:
                for l in range(2):
                    slot(t, l, 0)
            for i in range(EARLY_FROM // 2 * 2, N_LOOP):
                slot(i // 2, i % 2, EARLY_ADDS if i >= EARLY_FROM else 0)
            walk(tail)


def layouts(a):
    import numpy as np

    def up(w, c0):
        rows = w[c0:c0 + P]
        return np.transpose(rows.reshape(P, KD, P), (2, 1, 0)).reshape(P, KD * P)

    w_in, w_out = a["L0_attn_W_in"], a["L0_attn_W_out"]
    w_mix = np.stack([np.concatenate([up(w_in, c * P), up(w_in, 1024 + c * P), w_out[:, c * P:(c + 1) * P].T], 1)
                      for c in range(8)])
    w1, w2 = a["L0_attn_W_mlp1"], a["L0_attn_W_mlp2"]
    w_mlp = np.stack([np.concatenate([up(w1, 2 * c * P), up(w1, (2 * c + 1) * P)]
                                     + [w2[:, r * P:(r + 1) * P].T for r in (2 * c, 2 * c + 1)], 1)
                      for c in range(8)])

    def expert_units(u1, u3, u2, c1, c3):
        fill = -u1.shape[0] % P
        u1, u3, u2, c1, c3 = (np.concatenate([v, np.zeros((fill,) + v.shape[1:], v.dtype)], 0)
                              for v in (u1, u3, u2, c1, c3))
        return np.stack([np.concatenate([up(u1, r), up(u3, r), u2[r:r + P], c1[r:r + P, None], c3[r:r + P, None]], 1)
                         for r in range(0, u1.shape[0], P)])

    w_shared = expert_units(a["L0_ffn_ws1"], a["L0_ffn_ws3"], a["L0_ffn_ws2"].T, a["L0_ffn_bs1"], a["L0_ffn_bs3"])
    w_moe = np.concatenate([expert_units(a["L0_ffn_w1"][e], a["L0_ffn_w3"][e], a["L0_ffn_w2"][e].T, a["L0_ffn_b1"][e],
                                         a["L0_ffn_b3"][e]) for e in range(E)], 0)
    conv = np.concatenate([a["L0_attn_conv_w"][:, 0, :], a["L0_attn_conv_b"][:, None]], 1)
    conv = np.transpose(conv.reshape(8, P, TAPS + 1), (1, 0, 2))
    gate_w = np.transpose(a["L0_ffn_gate_w"].reshape(E, KD, P), (2, 1, 0))
    out_bias = np.concatenate([a["L0_ffn_b2"], a["L0_ffn_bs2"][None]], 0)
    return {"x": a["L0_attn_x"].reshape(T, D), "w_mix": w_mix, "w_mlp": w_mlp, "w_shared": w_shared, "w_moe": w_moe,
            "conv": conv, "gate_w": gate_w, "gate_b": a["L0_ffn_gate_b"], "out_bias": out_bias}


def kernel(**inputs):
    import numpy as np
    import concourse.bacc as bacc
    from concourse.bass_utils import run_bass_kernel_spmd

    arrays = {n: np.ascontiguousarray(v) for n, v in layouts({n: np.asarray(v) for n, v in inputs.items()}).items()}
    nc = bacc.Bacc("TRN2", target_bir_lowering=False, num_devices=1)
    args = [nc.dram_tensor(n, v.shape, F32, kind="ExternalInput").ap() for n, v in arrays.items()]
    args.append(nc.dram_tensor("out", (T, D), F32, kind="ExternalOutput").ap())
    layer(nc, *args)
    got = run_bass_kernel_spmd(nc, [arrays], core_ids=[0])
    return got.results[0]["out"].reshape(NB, TB, D)
```
